# Optimizing a Trainium2 kernel written in Bass

```python
import numpy as np
import jax
import jax.numpy as jnp

def _softmax(x, axis=-1):
    return jax.nn.softmax(x, axis=axis)

def _gelu(x):
    return jax.nn.gelu(x, approximate=True)

def _silu(x):
    return jax.nn.silu(x)

def _sigmoid(x):
    return jax.nn.sigmoid(x)

def _layernorm(x, axis=-1, eps=1e-05):
    m = jnp.mean(x, axis=axis, keepdims=True)
    v = jnp.var(x, axis=axis, keepdims=True)
    return (x - m) / jnp.sqrt(v + eps)

def _scatter_add(tgt, idx, src, axis=0):
    return tgt.at[idx].add(src)

def _segment_sum(src, seg, n):
    return jax.ops.segment_sum(src, seg, n)
kernel_name = 'mk_dlrm_tower_d1_rec_r8_217162'

def setup_inputs(seed: int=0):
    np.random.seed(seed)
    _w = jnp.asarray

    def _rec_inputs():
        import jax
        import jax.numpy as jnp
        _tk = jax.random.key(seed)
        ids = jnp.stack([jax.random.randint(jax.random.fold_in(_tk, 200 + f), (2048,), 0, v, jnp.int32) for f, v in enumerate([125000, 12500, 1000, 1250, 1000, 1000, 1000, 12500, 1250, 12500, 1000, 12500, 1250, 1250, 12500, 1250, 1250, 1250, 1250, 12500, 12500, 12500, 1250, 1000, 1000, 1000])], axis=1)
        tbl_0 = 0.05 * jax.random.normal(jax.random.fold_in(_tk, 500 + 0), (125000, 128), jnp.float32)
        tbl_1 = 0.05 * jax.random.normal(jax.random.fold_in(_tk, 500 + 1), (12500, 128), jnp.float32)
        tbl_2 = 0.05 * jax.random.normal(jax.random.fold_in(_tk, 500 + 2), (1000, 128), jnp.float32)
        tbl_3 = 0.05 * jax.random.normal(jax.random.fold_in(_tk, 500 + 3), (1250, 128), jnp.float32)
        tbl_4 = 0.05 * jax.random.normal(jax.random.fold_in(_tk, 500 + 4), (1000, 128), jnp.float32)
        tbl_5 = 0.05 * jax.random.normal(jax.random.fold_in(_tk, 500 + 5), (1000, 128), jnp.float32)
        tbl_6 = 0.05 * jax.random.normal(jax.random.fold_in(_tk, 500 + 6), (1000, 128), jnp.float32)
        tbl_7 = 0.05 * jax.random.normal(jax.random.fold_in(_tk, 500 + 7), (12500, 128), jnp.float32)
        tbl_8 = 0.05 * jax.random.normal(jax.random.fold_in(_tk, 500 + 8), (1250, 128), jnp.float32)
        tbl_9 = 0.05 * jax.random.normal(jax.random.fold_in(_tk, 500 + 9), (12500, 128), jnp.float32)
        tbl_10 = 0.05 * jax.random.normal(jax.random.fold_in(_tk, 500 + 10), (1000, 128), jnp.float32)
        tbl_11 = 0.05 * jax.random.normal(jax.random.fold_in(_tk, 500 + 11), (12500, 128), jnp.float32)
        tbl_12 = 0.05 * jax.random.normal(jax.random.fold_in(_tk, 500 + 12), (1250, 128), jnp.float32)
        tbl_13 = 0.05 * jax.random.normal(jax.random.fold_in(_tk, 500 + 13), (1250, 128), jnp.float32)
        tbl_14 = 0.05 * jax.random.normal(jax.random.fold_in(_tk, 500 + 14), (12500, 128), jnp.float32)
        tbl_15 = 0.05 * jax.random.normal(jax.random.fold_in(_tk, 500 + 15), (1250, 128), jnp.float32)
        tbl_16 = 0.05 * jax.random.normal(jax.random.fold_in(_tk, 500 + 16), (1250, 128), jnp.float32)
        tbl_17 = 0.05 * jax.random.normal(jax.random.fold_in(_tk, 500 + 17), (1250, 128), jnp.float32)
        tbl_18 = 0.05 * jax.random.normal(jax.random.fold_in(_tk, 500 + 18), (1250, 128), jnp.float32)
        tbl_19 = 0.05 * jax.random.normal(jax.random.fold_in(_tk, 500 + 19), (12500, 128), jnp.float32)
        tbl_20 = 0.05 * jax.random.normal(jax.random.fold_in(_tk, 500 + 20), (12500, 128), jnp.float32)
        tbl_21 = 0.05 * jax.random.normal(jax.random.fold_in(_tk, 500 + 21), (12500, 128), jnp.float32)
        tbl_22 = 0.05 * jax.random.normal(jax.random.fold_in(_tk, 500 + 22), (1250, 128), jnp.float32)
        tbl_23 = 0.05 * jax.random.normal(jax.random.fold_in(_tk, 500 + 23), (1000, 128), jnp.float32)
        tbl_24 = 0.05 * jax.random.normal(jax.random.fold_in(_tk, 500 + 24), (1000, 128), jnp.float32)
        tbl_25 = 0.05 * jax.random.normal(jax.random.fold_in(_tk, 500 + 25), (1000, 128), jnp.float32)
        _rk = jax.random.fold_in(_tk, 7)
        r_dense_features = -0.000520686 + 1.00062 * jax.random.normal(jax.random.fold_in(_rk, 101), (2048, 128), jnp.float32)
        W_top1 = 0.0405887 * jax.random.normal(jax.random.fold_in(_tk, 801), (607, 512), jnp.float32)
        W_top2 = 0.0441942 * jax.random.normal(jax.random.fold_in(_tk, 802), (512, 256), jnp.float32)
        W_top3 = 0.0625 * jax.random.normal(jax.random.fold_in(_tk, 803), (256, 1), jnp.float32)
        b_top1 = jnp.zeros((512,), jnp.float32)
        b_top2 = jnp.zeros((256,), jnp.float32)
        return (r_dense_features, ids, tbl_0, tbl_1, tbl_2, tbl_3, tbl_4, tbl_5, tbl_6, tbl_7, tbl_8, tbl_9, tbl_10, tbl_11, tbl_12, tbl_13, tbl_14, tbl_15, tbl_16, tbl_17, tbl_18, tbl_19, tbl_20, tbl_21, tbl_22, tbl_23, tbl_24, tbl_25, W_top1, b_top1, W_top2, b_top2, W_top3)
    r_dense_features, ids, tbl_0, tbl_1, tbl_2, tbl_3, tbl_4, tbl_5, tbl_6, tbl_7, tbl_8, tbl_9, tbl_10, tbl_11, tbl_12, tbl_13, tbl_14, tbl_15, tbl_16, tbl_17, tbl_18, tbl_19, tbl_20, tbl_21, tbl_22, tbl_23, tbl_24, tbl_25, W_top1, b_top1, W_top2, b_top2, W_top3 = _rec_inputs()

    def _L0_rec_setup():
        import jax, jax.numpy as jnp
        import numpy as np
        NUM_SPARSE = 26
        EMBED_DIM = 128
        BATCH = 2048
        key = jax.random.key(seed)
        k1, k2 = jax.random.split(key)
        dense_features = jax.random.normal(k1, (BATCH, EMBED_DIM), dtype=jnp.float32)
        sparse_features = jax.random.normal(k2, (BATCH, NUM_SPARSE, EMBED_DIM), dtype=jnp.float32)
        return {'dense_features': dense_features, 'sparse_features': sparse_features}
    _L0_rec_all = _L0_rec_setup()
    _L0_rec_in = {k: v for k, v in _L0_rec_all.items() if k in ()}
    del _L0_rec_all
    return {'r_dense_features': r_dense_features, 'ids': ids, 'tbl_0': tbl_0, 'tbl_1': tbl_1, 'tbl_2': tbl_2, 'tbl_3': tbl_3, 'tbl_4': tbl_4, 'tbl_5': tbl_5, 'tbl_6': tbl_6, 'tbl_7': tbl_7, 'tbl_8': tbl_8, 'tbl_9': tbl_9, 'tbl_10': tbl_10, 'tbl_11': tbl_11, 'tbl_12': tbl_12, 'tbl_13': tbl_13, 'tbl_14': tbl_14, 'tbl_15': tbl_15, 'tbl_16': tbl_16, 'tbl_17': tbl_17, 'tbl_18': tbl_18, 'tbl_19': tbl_19, 'tbl_20': tbl_20, 'tbl_21': tbl_21, 'tbl_22': tbl_22, 'tbl_23': tbl_23, 'tbl_24': tbl_24, 'tbl_25': tbl_25, 'W_top1': W_top1, 'b_top1': b_top1, 'W_top2': W_top2, 'b_top2': b_top2, 'W_top3': W_top3}

def reference(r_dense_features, ids, tbl_0, tbl_1, tbl_2, tbl_3, tbl_4, tbl_5, tbl_6, tbl_7, tbl_8, tbl_9, tbl_10, tbl_11, tbl_12, tbl_13, tbl_14, tbl_15, tbl_16, tbl_17, tbl_18, tbl_19, tbl_20, tbl_21, tbl_22, tbl_23, tbl_24, tbl_25, W_top1, b_top1, W_top2, b_top2, W_top3):
    import jax
    import jax.numpy as jnp

    def _L0_rec_ref(dense_features, sparse_features):
        import jax, jax.numpy as jnp
        import numpy as np
        NUM_SPARSE = 26
        EMBED_DIM = 128
        BATCH = 2048
        F = NUM_SPARSE + 1
        combined = jnp.concatenate([dense_features[:, None, :], sparse_features], axis=1)
        interactions = jnp.einsum('bfd,bgd->bfg', combined, combined)
        iu, ju = jnp.triu_indices(F, k=1)
        interactions_flat = interactions[:, iu, ju]
        return jnp.concatenate([dense_features, interactions_flat], axis=1)
    e = jnp.stack([tbl_0[ids[:, 0]], tbl_1[ids[:, 1]], tbl_2[ids[:, 2]], tbl_3[ids[:, 3]], tbl_4[ids[:, 4]], tbl_5[ids[:, 5]], tbl_6[ids[:, 6]], tbl_7[ids[:, 7]], tbl_8[ids[:, 8]], tbl_9[ids[:, 9]], tbl_10[ids[:, 10]], tbl_11[ids[:, 11]], tbl_12[ids[:, 12]], tbl_13[ids[:, 13]], tbl_14[ids[:, 14]], tbl_15[ids[:, 15]], tbl_16[ids[:, 16]], tbl_17[ids[:, 17]], tbl_18[ids[:, 18]], tbl_19[ids[:, 19]], tbl_20[ids[:, 20]], tbl_21[ids[:, 21]], tbl_22[ids[:, 22]], tbl_23[ids[:, 23]], tbl_24[ids[:, 24]], tbl_25[ids[:, 25]]], axis=1)
    z = _L0_rec_ref(r_dense_features, e)
    z = z.reshape(z.shape[0], -1)
    h = jnp.concatenate([z, r_dense_features], axis=1)
    h = jnp.maximum(h @ W_top1 + b_top1, 0.0)
    h = jnp.maximum(h @ W_top2 + b_top2, 0.0)
    y = h @ W_top3
    return y

_drawn_inputs = setup_inputs


def setup_inputs(seed=0):
    import zlib

    import numpy as np

    out = dict(_drawn_inputs(seed))
    spreads = {'b_top1': (0.0, 0.1), 'b_top2': (0.0, 0.1)}
    factors = {}
    for name, (base, spread) in spreads.items():
        noise = np.random.default_rng([zlib.crc32(name.encode()), seed]).standard_normal(out[name].shape)
        drawn = base * np.exp(spread * noise) if base else spread * noise
        out[name] = jnp.asarray(drawn.astype(out[name].dtype))
    for name, factor in factors.items():
        out[name] = (out[name] * factor).astype(out[name].dtype)
    return out
```

```python
import concourse.bass as bass
from concourse import mybir
from contextlib import ExitStack

BATCH = 2048
P = 128
NUM_TABLES = 26
F = NUM_TABLES + 1
PAIRS = F * (F - 1) // 2
LOOKED_UP = (2, 4, 5, 6, 10, 23)
GATHERED = tuple(f for f in range(NUM_TABLES) if f not in LOOKED_UP)
ORDER = (0,) + tuple(1 + f for f in GATHERED + LOOKED_UP)
X = len(LOOKED_UP)
NG = len(GATHERED)
NT = 1 + NG
ROWS = 1000
KT = 8
KP = ROWS // KT

TILES = 4
GROUPS = BATCH // (P * TILES)
GS = P * TILES
XC = X // 2
PAIR_SAMPLES = 2 * P
TB = 4
NB = -(-NT // TB)
QB = 4
GB = P // (4 * QB)
FS = 32
H1, H2 = 512, 256
H1C, H2C = H1 // P, H2 // P
ZC = [(c, min(P, PAIRS - c)) for c in range(0, PAIRS, P)]
CB = [list(range(i, min(i + TB, F - 1))) for i in range(0, F - 1, TB)]
USE_D = len(CB)
USE_L1 = USE_D + len(ZC)
USE_L2 = USE_L1 + H1C
USE_L3 = USE_L2 + H2C
USES = USE_L3 + 1
PAIR_AT = [sum(F - 1 - k for k in range(i)) for i in range(F)]


def same_bank_before(use):
    bank = mlp_bank(use)
    u = use - 1
    while (mlp_bank(u) if u >= 0 else mlp_bank(u + USES)) != bank:
        u -= 1
    return u


def mlp_bank(use):
    return use % 2


def dlrm_kernel(nc, dense, ids_tiles, ids_rows, gathered_tables, looked_up_tables, w1, b1, w2, b2, w3,
                identity_c, row_numbers_c, out):
    f32 = mybir.dt.float32
    f32r = mybir.dt.float32r
    i32 = mybir.dt.int32
    ALU = mybir.AluOpType
    RELU = mybir.ActivationFunctionType.Relu

    ctx = ExitStack()
    with ctx:
        def sb(name, shape, dt=f32):
            return ctx.enter_context(nc.sbuf_tensor(name, shape, dt))

        def sem(name):
            return ctx.enter_context(nc.semaphore(name))

        identity = sb("identity", [P, P])
        row_numbers = sb("row_numbers", [KP, KT])
        indices = sb("indices", [P, TILES, NUM_TABLES], i32)
        ids_of_chunk = sb("ids_of_chunk", [P, XC * PAIR_SAMPLES], i32)
        rows = sb("rows", [P, 2, NT, P])
        table_hi = sb("table_hi", [KP, X, KT * P], f32r)
        table_lo = sb("table_lo", [KP, X, KT * P], f32r)
        onehot = sb("onehot", [KP, KT, XC * PAIR_SAMPLES], f32r)
        rows_t = sb("rows_t", [P, TILES, P, FS])
        dots = sb("dots", [P, P, F])
        dense_t = sb("dense_t", [P, 2, 4, P])
        pairs = sb("pairs", [P, 4, H1])
        pairs_t = sb("pairs_t", [P, len(ZC), GS])
        w1_sb = sb("w1_sb", [P, 1 + len(ZC), H1])
        w2_sb = sb("w2_sb", [P, H1C, H2])
        w3_sb = sb("w3_sb", [P, H2C])
        b1_sb = sb("b1_sb", [P, H1C])
        b2_sb = sb("b2_sb", [P, H2C])
        y_sb = sb("y_sb", [1, GS])
        h1_t = pairs
        h2_t = pairs_t
        w1_dense2 = pairs_t[:, 0, :]
        STAGED = 3
        staged = [dots[:, :, :].rearrange("p q f -> p (q f)")[0:KP, s * KT * P:(s + 1) * KT * P]
                  for s in range(STAGED)]

        def bank(name):
            return ctx.enter_context(nc.psum_tensor(name, [P, 512], f32))

        transpose_banks = [bank(f"transpose_bank{i}") for i in range(2)]
        lookup_banks = [bank(f"lookup_bank{i}") for i in range(2)]
        dots_banks = [bank(f"dots_bank{i}") for i in range(2)]
        mlp_banks = [bank(f"mlp_bank{i}") for i in range(2)]

        identity_loaded = sem("identity_loaded")
        numbers_loaded = sem("numbers_loaded")
        weights_loaded = sem("weights_loaded")
        table_staged = [sem(f"table_staged{s}") for s in range(STAGED)]
        hi_made = sem("hi_made")
        lo_made = sem("lo_made")
        padding_cleared = sem("padding_cleared")
        dense_weights_summed = sem("dense_weights_summed")
        indices_loaded = [sem(f"indices_loaded{t}") for t in range(TILES)]
        ids_loaded = sem("ids_loaded")
        dense_loaded = [sem(f"dense_loaded{s}") for s in range(2)]
        gathered = [[sem(f"gathered{s}_{b}") for b in range(NB)] for s in range(2)]
        gathers_begun = sem("gathers_begun")
        onehot_made = sem("onehot_made")
        lookup_done = sem("lookup_done")
        lookup_stored = sem("lookup_stored")
        transposed = sem("transposed")
        transposed_stored = sem("transposed_stored")
        dense_stored = sem("dense_stored")
        dots_done = sem("dots_done")
        dots_stored_act = sem("dots_stored_act")
        dots_stored_dve = sem("dots_stored_dve")
        mlp_done = sem("mlp_done")
        mlp_stored = sem("mlp_stored")
        out_stored = sem("out_stored")

        def tile_of(g, t):
            return g * TILES + t

        def chunk_end(tile):
            return (tile + 1) * XC

        def rows_t_of(tile_slot):
            return rows_t[:, tile_slot, :, :].rearrange("p s f -> p f s")

        block = ctx.enter_context(nc.Block())

        @block.sync
        def _(sp):
            def load_tile(g, t, first):
                tile = tile_of(g, t)
                s = t % 2
                if not first:
                    sp.wait_ge(transposed, (tile - 3) * NB)
                sp.dma_start(indices[:, t, :], ids_tiles[bass.ds(tile, 1), :, :].rearrange("a p f -> p (a f)")
                             ).then_inc(indices_loaded[t], 16)
                if not (first and t < 2):
                    sp.wait_ge(transposed, (tile - 1) * NB)
                sp.dma_start(rows[:, s, 0, :], dense[bass.ds(tile * P, P), :]).then_inc(dense_loaded[s], 16)
                if not (first and t == 0):
                    sp.wait_ge(onehot_made, tile)
                sp.dma_start(
                    ids_of_chunk[:, :].rearrange("p (x n) -> p x n", x=XC),
                    ids_rows[s * XC:(s + 1) * XC, bass.ds(g * GS + (t // 2) * PAIR_SAMPLES, PAIR_SAMPLES)]
                    .partition_broadcast(P)).then_inc(ids_loaded, 16)

            def stage_table(x):
                if x >= STAGED:
                    sp.wait_ge(lo_made, x - STAGED + 1)
                full = KP // 16 * 16
                src = looked_up_tables[x].rearrange("(p k) d -> p (k d)", k=KT)
                sp.dma_start(staged[x % STAGED][0:full, :], src[0:full, :]).then_inc(table_staged[x % STAGED], 16)
                sp.dma_start(staged[x % STAGED][full:KP, :], src[full:KP, :]).then_inc(table_staged[x % STAGED], 16)

            load_tile(0, 0, True)
            sp.dma_start(row_numbers[:], row_numbers_c).then_inc(numbers_loaded, 16)
            for x in range(STAGED):
                stage_table(x)
            sp.dma_start(identity[:], identity_c).then_inc(identity_loaded, 16)
            for x in range(STAGED, X):
                stage_table(x)
            load_tile(0, 1, True)
            sp.dma_start(w1_sb[:, 0, :], w1[0:P, :]).then_inc(weights_loaded, 16)
            sp.dma_start(w1_dense2, w1[P:2 * P, :]).then_inc(weights_loaded, 16)
            for c, (at, n) in enumerate(ZC):
                sp.dma_start(w1_sb[0:n, 1 + c, :], w1[2 * P + at:2 * P + at + n, :]).then_inc(weights_loaded, 16)
            sp.dma_start(w2_sb[:], w2.rearrange("(c p) n -> p c n", p=P)).then_inc(weights_loaded, 16)
            sp.dma_start(w3_sb[:], w3).then_inc(weights_loaded, 16)
            sp.dma_start(b1_sb[:], b1).then_inc(weights_loaded, 16)
            sp.dma_start(b2_sb[:], b2).then_inc(weights_loaded, 16)
            for t in range(2, TILES):
                load_tile(0, t, True)
            with sp.Fori(1, GROUPS) as g:
                for t in range(TILES):
                    load_tile(g, t, False)

        WEIGHT_LOADS = 2 + len(ZC) + 4

        @block.gpsimd
        def _(pool):
            def gather_tile(g, t, first):
                tile = tile_of(g, t)
                s = t % 2
                pool.wait_ge(indices_loaded[t], (g + 1) * 16)
                if not (first and t < 2):
                    pool.wait_ge(transposed, (tile - 1) * NB)
                pool.sem_inc(gathers_begun, 1)
                for n, f in enumerate(GATHERED):
                    nc.gpsimd.indirect_dma_start(
                        rows[:, s, 1 + n, :], None, gathered_tables[n],
                        bass.IndirectOffsetOnAxis(indices[:, t, f:f + 1], 0)).then_inc(gathered[s][(1 + n) // TB], 16)

            for t in range(TILES):
                gather_tile(0, t, True)
            with pool.Fori(1, GROUPS) as g:
                for t in range(TILES):
                    gather_tile(g, t, False)

        @block.tensor
        def _(pe):
            def look_up(g, t):
                tile = tile_of(g, t)
                pe.wait_ge(onehot_made, tile + 1)
                for c in range(XC):
                    x = (t % 2) * XC + c
                    u = t * XC + c
                    if not (isinstance(g, int) and g == 0 and u < 2):
                        pe.wait_ge(lookup_stored, tile * XC + c - 1)
                    into = lookup_banks[u % 2][:, 0:PAIR_SAMPLES]
                    ids = onehot[:, :, c * PAIR_SAMPLES:(c + 1) * PAIR_SAMPLES]
                    for k in range(KT):
                        for half in (table_hi, table_lo):
                            last = nc.tensor.matmul(into, half[:, x, k * P:(k + 1) * P], ids[:, k, :],
                                                    start=(k == 0 and half is table_hi),
                                                    stop=(k == KT - 1 and half is table_lo))
                    last.then_inc(lookup_done, 1)

            def transpose_rows(g, t):
                tile = tile_of(g, t)
                s = t % 2
                pe.wait_ge(dense_loaded[s], (g * 2 + t // 2 + 1) * 16)
                for b in range(NB):
                    features = range(b * TB, min(NT, (b + 1) * TB))
                    pe.wait_ge(gathered[s][b], (g * 2 + t // 2 + 1) * 16 * (len(features) - (b == 0)))
                    u = t * NB + b
                    if not (isinstance(g, int) and g == 0 and u < 2):
                        pe.wait_ge(transposed_stored, tile * NB + b - 1)
                    for i, f in enumerate(features):
                        last = nc.tensor.transpose(transpose_banks[u % 2][:, i * P:(i + 1) * P],
                                                   rows[:, s, f, :], identity[:])
                    last.then_inc(transposed, 1)

            def dot_products(g, t, first=False):
                tile = tile_of(g, t)
                pe.wait_ge(transposed_stored, (tile + 1) * NB)
                pe.wait_ge(lookup_stored, (tile - t % 2 + 2) * XC)
                quads = rows_t[:, t, :, :].rearrange("p (q j) f -> p q j f", j=4)
                for i in range(GB):
                    if not (first and i < 2):
                        pe.wait_ge(dots_stored_act, tile * GB + i - 1)
                        pe.wait_ge(dots_stored_dve, tile * GB + i - 1)
                    for b in range(QB):
                        quad = quads[:, i * QB + b, :, :]
                        last = nc.tensor.matmul(dots_banks[i % 2][:, b * 4 * F:(b + 1) * 4 * F],
                                                quad.rearrange("p j f -> p (j f)"), quad[:, :, 0:F],
                                                start=True, stop=True)
                    last.then_inc(dots_done, 1)

            def claim(g, use):
                before = same_bank_before(use)
                if before >= 0:
                    pe.wait_ge(mlp_stored, g * USES + before + 1)
                return mlp_banks[mlp_bank(use)]

            def stage_c(g):
                pe.wait_ge(dots_stored_act, (g + 1) * TILES * GB)
                pe.wait_ge(dots_stored_dve, (g + 1) * TILES * GB)
                for n, features in enumerate(CB):
                    into = claim(g, n)
                    for k, i in enumerate(features):
                        last = nc.tensor.transpose(into[:, k * P:(k + 1) * P], dots[:, :, i], identity[:])
                    last.then_inc(mlp_done, 1)

            def stage_d(g):
                pe.wait_ge(mlp_stored, g * USES + USE_D)
                for c, (at, n) in enumerate(ZC):
                    into = claim(g, USE_D + c)
                    for j in range(4):
                        last = nc.tensor.transpose(into[0:n, j * P:(j + 1) * P], pairs[:, j, at:at + n],
                                                   identity[:])
                    last.then_inc(mlp_done, 1)

            def layer_1(g):
                pe.wait_ge(mlp_stored, g * USES + USE_L1)
                pe.wait_ge(dense_stored, (g + 1) * TILES)
                for m in range(H1C):
                    into = claim(g, USE_L1 + m)
                    nc.tensor.matmul(into[:], w1_sb[:, 0, m * P:(m + 1) * P],
                                     dense_t[:, bass.ds(g % 2, 1), :, :].rearrange("p g j q -> p (g j q)"),
                                     start=True, stop=False)
                    for c, (_, n) in enumerate(ZC):
                        last = nc.tensor.matmul(into[:], w1_sb[0:n, 1 + c, m * P:(m + 1) * P],
                                                pairs_t[0:n, c, :], start=False, stop=(c == len(ZC) - 1))
                    last.then_inc(mlp_done, 1)

            def layer_2(g):
                pe.wait_ge(mlp_stored, g * USES + USE_L2)
                for m in range(H2C):
                    into = claim(g, USE_L2 + m)
                    for c in range(H1C):
                        last = nc.tensor.matmul(into[:], w2_sb[:, c, m * P:(m + 1) * P], h1_t[:, c, :],
                                                start=(c == 0), stop=(c == H1C - 1))
                    last.then_inc(mlp_done, 1)

            def layer_3(g):
                pe.wait_ge(mlp_stored, g * USES + USE_L3)
                into = claim(g, USE_L3)
                for c in range(H2C):
                    last = nc.tensor.matmul(into[0:1, :], w3_sb[:, c:c + 1], h2_t[:, c, :],
                                            start=(c == 0), stop=(c == H2C - 1))
                last.then_inc(mlp_done, 1)

            pe.wait_ge(lo_made, X)
            pe.wait_ge(hi_made, X)
            pe.wait_ge(identity_loaded, 16)
            pe.wait_ge(padding_cleared, 1)
            pe.wait_ge(dense_weights_summed, 1)
            pe.wait_ge(weights_loaded, WEIGHT_LOADS * 16)
            for t in range(TILES):
                look_up(0, t)
                transpose_rows(0, t)
                if t > 0:
                    dot_products(0, t - 1, first=(t == 1))
            with pe.Fori(1, GROUPS) as g:
                look_up(g, 0)
                transpose_rows(g, 0)
                dot_products(g - 1, 3)
                look_up(g, 1)
                stage_c(g - 1)
                transpose_rows(g, 1)
                dot_products(g, 0)
                stage_d(g - 1)
                look_up(g, 2)
                layer_1(g - 1)
                transpose_rows(g, 2)
                dot_products(g, 1)
                layer_2(g - 1)
                look_up(g, 3)
                layer_3(g - 1)
                transpose_rows(g, 3)
                dot_products(g, 2)
                pe.wait_ge(mlp_stored, g * USES)
            dot_products(GROUPS - 1, 3)
            stage_c(GROUPS - 1)
            stage_d(GROUPS - 1)
            layer_1(GROUPS - 1)
            layer_2(GROUPS - 1)
            layer_3(GROUPS - 1)

        ACT_BLOCKS = (0, 1, 2)
        DVE_BLOCKS = (3,)

        def dots_block(i, j):
            return dots_banks[i % 2][32 * j:32 * j + 32, 0:QB * 4 * F].rearrange(
                "p (b j f) -> p b j f", j=4, f=F)[:, :, j, :]

        @block.scalar
        def _(act):
            def store_look_ups(g, t):
                tile = tile_of(g, t)
                for c in range(XC):
                    u = t * XC + c
                    f = NT + (t % 2) * XC + c
                    act.wait_ge(lookup_done, tile * XC + c + 1)
                    pair = rows_t[:, t - t % 2:t - t % 2 + 2, :, :]
                    nc.scalar.copy(pair[:, :, :, f],
                                   lookup_banks[u % 2][:, 0:PAIR_SAMPLES].rearrange("p (a s) -> p a s", a=2)
                                   ).then_inc(lookup_stored, 1)

            def store_transposed(g, t):
                tile = tile_of(g, t)
                for b in range(NB):
                    n = min(NT, (b + 1) * TB) - b * TB
                    into = transpose_banks[(t * NB + b) % 2]
                    act.wait_ge(transposed, tile * NB + b + 1)
                    if b == 0:
                        nc.scalar.copy(
                            dense_t[:, bass.ds(g % 2, 1), :, t * 32:(t + 1) * 32].rearrange("p g j q -> p q (g j)"),
                            into[:, 0:P].rearrange("p (q j) -> p q j", j=4)).then_inc(dense_stored, 1)
                    nc.scalar.copy(rows_t_of(t)[:, b * TB:b * TB + n, :],
                                   into[:, 0:n * P].rearrange("p (f s) -> p f s", f=n)
                                   ).then_inc(transposed_stored, 1)

            def store_dots(g, t):
                tile = tile_of(g, t)
                for i in range(GB):
                    act.wait_ge(dots_done, tile * GB + i + 1)
                    q = t * 32 + i * QB
                    for j in ACT_BLOCKS:
                        last = nc.scalar.copy(dots[32 * j:32 * j + 32, q:q + QB, :], dots_block(i, j))
                    last.then_inc(dots_stored_act, 1)

            def store_layer_1(g):
                for m in range(H1C):
                    act.wait_ge(mlp_done, g * USES + USE_L1 + m + 1)
                    nc.scalar.activation(h1_t[:, m, :], mlp_banks[mlp_bank(USE_L1 + m)][:], RELU,
                                         bias=b1_sb[:, m:m + 1]).then_inc(mlp_stored, 1)

            def store_layer_2(g):
                for m in range(H2C):
                    act.wait_ge(mlp_done, g * USES + USE_L2 + m + 1)
                    nc.scalar.activation(h2_t[:, m, :], mlp_banks[mlp_bank(USE_L2 + m)][:], RELU,
                                         bias=b2_sb[:, m:m + 1]).then_inc(mlp_stored, 1)

            def store_layer_3(g):
                act.wait_ge(mlp_done, g * USES + USES)
                nc.scalar.copy(y_sb[0:1, :].rearrange("p (q j) -> p j q", j=4),
                               mlp_banks[mlp_bank(USE_L3)][0:1, :].rearrange("p (j q) -> p j q", j=4)
                               ).then_inc(mlp_stored, 1)
                act.wait_ge(mlp_stored, g * USES + USES)
                act.dma_start(out[0:1, bass.ds(g * GS, GS)], y_sb[:]).then_inc(out_stored, 16)

            for x in range(X):
                act.wait_ge(table_staged[x % STAGED], (x // STAGED + 1) * 32)
                nc.scalar.copy(table_hi[:, x, :], staged[x % STAGED]).then_inc(hi_made, 1)
            act.wait_ge(weights_loaded, WEIGHT_LOADS * 16)
            for t in range(TILES):
                store_look_ups(0, t)
                store_transposed(0, t)
                if t > 0:
                    store_dots(0, t - 1)
            with act.Fori(1, GROUPS) as g:
                store_look_ups(g, 0)
                store_transposed(g, 0)
                store_dots(g - 1, 3)
                store_look_ups(g, 1)
                store_transposed(g, 1)
                store_dots(g, 0)
                store_look_ups(g, 2)
                store_layer_1(g - 1)
                store_transposed(g, 2)
                store_dots(g, 1)
                store_layer_2(g - 1)
                store_look_ups(g, 3)
                store_layer_3(g - 1)
                store_transposed(g, 3)
                store_dots(g, 2)
                act.wait_ge(out_stored, g * 16)
            store_dots(GROUPS - 1, 3)
            store_layer_1(GROUPS - 1)
            store_layer_2(GROUPS - 1)
            store_layer_3(GROUPS - 1)
            act.wait_ge(out_stored, GROUPS * 16)

        @block.vector
        def _(dve):
            def start_onehot(g, t, first=False):
                tile = tile_of(g, t)
                dve.wait_ge(ids_loaded, (tile + 1) * 16)
                if not first:
                    dve.wait_ge(lookup_done, tile * XC)

            def make_onehot(k):
                return nc.vector.tensor_scalar(onehot[:, k, :], ids_of_chunk[0:KP, :],
                                               row_numbers[:, k:k + 1], None, ALU.is_equal)

            def store_dots(g, t, i):
                tile = tile_of(g, t)
                dve.wait_ge(dots_done, tile * GB + i + 1)
                q = t * 32 + i * QB
                for j in DVE_BLOCKS:
                    last = nc.vector.tensor_copy(dots[32 * j:32 * j + 32, q:q + QB, :], dots_block(i, j))
                last.then_inc(dots_stored_dve, 1)

            def step(g, t, dots_of, first=False):
                start_onehot(g, t, first)
                AHEAD = 2
                for k in range(AHEAD):
                    make_onehot(k)
                for i in range(GB):
                    if dots_of is not None:
                        store_dots(*dots_of, i)
                    if i + AHEAD < KT:
                        last = make_onehot(i + AHEAD)
                last.then_inc(onehot_made, 1)

            def store_stage_c(g):
                for n, features in enumerate(CB):
                    dve.wait_ge(mlp_done, g * USES + n + 1)
                    into = mlp_banks[mlp_bank(n)]
                    for k, i in enumerate(features):
                        after = into[:, k * P:(k + 1) * P].rearrange("p (j f) -> p j f", j=4)[:, :, i + 1:F]
                        last = nc.vector.tensor_copy(pairs[:, :, PAIR_AT[i]:PAIR_AT[i + 1]], after)
                    last.then_inc(mlp_stored, 1)

            def store_stage_d(g):
                for c, (_, n) in enumerate(ZC):
                    dve.wait_ge(mlp_done, g * USES + USE_D + c + 1)
                    nc.vector.tensor_copy(pairs_t[0:n, c, :], mlp_banks[mlp_bank(USE_D + c)][0:n, :]
                                          ).then_inc(mlp_stored, 1)

            nc.vector.memset(rows_t[:, :, :, F:FS], 0.0).then_inc(padding_cleared, 1)
            for x in range(X):
                dve.wait_ge(table_staged[x % STAGED], (x // STAGED + 1) * 32)
                dve.wait_ge(hi_made, x + 1)
                nc.vector.tensor_tensor(table_lo[:, x, :], staged[x % STAGED], table_hi[:, x, :].bitcast(f32),
                                        ALU.subtract).then_inc(lo_made, 1)
            dve.wait_ge(numbers_loaded, 16)
            step(0, 0, None, first=True)
            dve.wait_ge(weights_loaded, WEIGHT_LOADS * 16)
            nc.vector.tensor_tensor(w1_sb[:, 0, :], w1_sb[:, 0, :], w1_dense2, ALU.add
                                    ).then_inc(dense_weights_summed, 1)
            step(0, 1, None)
            step(0, 2, (0, 0))
            step(0, 3, (0, 1))
            with dve.Fori(1, GROUPS) as g:
                step(g, 0, (g - 1, 2))
                step(g, 1, (g - 1, 3))
                store_stage_c(g - 1)
                step(g, 2, (g, 0))
                store_stage_d(g - 1)
                step(g, 3, (g, 1))
            for t in (2, 3):
                for i in range(GB):
                    store_dots(GROUPS - 1, t, i)
            store_stage_c(GROUPS - 1)
            store_stage_d(GROUPS - 1)


def kernel(**inputs):
    import numpy as np
    import concourse.bacc as bacc
    from concourse.bass_utils import run_bass_kernel_spmd

    def pair_row(i, j):
        a, b = sorted((ORDER[i], ORDER[j]))
        return P + a * (F - 1) - a * (a - 1) // 2 + b - a - 1

    w1_rows = list(range(P)) + list(range(P + PAIRS, P + PAIRS + P))
    w1_rows += [pair_row(i, j) for i in range(F) for j in range(i + 1, F)]
    ids = np.asarray(inputs["ids"])
    arrays = {
        "dense": np.asarray(inputs["r_dense_features"]),
        "ids_tiles": ids.reshape(BATCH // P, P, NUM_TABLES),
        "ids_rows": ids.T[list(LOOKED_UP)],
        "w1": np.asarray(inputs["W_top1"])[w1_rows],
        "b1": np.asarray(inputs["b_top1"]).reshape(H1C, P).T,
        "w2": np.asarray(inputs["W_top2"]),
        "b2": np.asarray(inputs["b_top2"]).reshape(H2C, P).T,
        "w3": np.asarray(inputs["W_top3"]).reshape(H2C, P).T,
        "identity": np.eye(P, dtype=np.float32),
        "row_numbers": np.arange(ROWS, dtype=np.float32).reshape(KP, KT),
    }
    for f in range(NUM_TABLES):
        arrays[f"tbl_{f}"] = np.asarray(inputs[f"tbl_{f}"])
    arrays = {k: np.ascontiguousarray(a) for k, a in arrays.items()}

    nc = bacc.Bacc("TRN2", target_bir_lowering=False, num_devices=1)
    ap = {k: nc.dram_tensor(f"in_{k}", a.shape, mybir.dt.from_np(a.dtype), kind="ExternalInput").ap()
          for k, a in arrays.items()}
    out = nc.dram_tensor("out", [1, BATCH], mybir.dt.float32, kind="ExternalOutput").ap()
    dlrm_kernel(nc, ap["dense"], ap["ids_tiles"], ap["ids_rows"], [ap[f"tbl_{f}"] for f in GATHERED],
                [ap[f"tbl_{f}"] for f in LOOKED_UP], ap["w1"], ap["b1"], ap["w2"], ap["b2"], ap["w3"],
                ap["identity"], ap["row_numbers"], out)
    result = run_bass_kernel_spmd(nc, [{f"in_{k}": a for k, a in arrays.items()}], core_ids=[0])
    return result.results[0]["out"].reshape(BATCH, 1)
```

```python
import concourse.bass as bass
from concourse import mybir
from contextlib import ExitStack

BATCH = 2048
P = 128
NUM_TABLES = 26
F = NUM_TABLES + 1
FM = F - 1
PAIRS = F * FM // 2
LOOKED_UP = (2, 4, 5, 6, 10, 23, 24)
GATHERED = tuple(f for f in range(NUM_TABLES) if f not in LOOKED_UP)
ORDER = (0,) + tuple(1 + f for f in GATHERED + LOOKED_UP)
X = len(LOOKED_UP)
NT = 1 + len(GATHERED)
ROWS = 1000
KT = 8
KP = ROWS // KT
B = 32

TILES = 4
GROUPS = BATCH // (P * TILES)
ALL_TILES = GROUPS * TILES
GS = P * TILES
QUADS = P // 4
PAIR_SAMPLES = 2 * P
CHUNKS = ((0, 1, 2, 3), (4, 5, 6))
HALF = 2
TB = 4
NB = NT // TB
QB = 4
GB = QUADS // QB
ZC = [(c, min(P, PAIRS - c)) for c in range(0, PAIRS, P)]
PAIR_AT = [sum(FM - k for k in range(i)) for i in range(F)]
H1, H2 = 512, 256
H1C, H2C = H1 // P, H2 // P
USE_L2 = H1C
USE_L3 = H1C + H2C
USES = USE_L3 + 1
assert NT % TB == 0 and NB % 2 == 1 and sum(len(c) for c in CHUNKS) == X


def counts(value):
    return not isinstance(value, int) or value > 0


def dlrm_kernel(nc, dense, ids_tiles, ids_rows, gathered_tables, looked_up_tables, w1, b1, w2, b2, w3,
                identity_c, row_numbers_c, out):
    f32 = mybir.dt.float32
    f32r = mybir.dt.float32r
    i32 = mybir.dt.int32
    ALU = mybir.AluOpType
    RELU = mybir.ActivationFunctionType.Relu

    ctx = ExitStack()
    with ctx:
        def sb(name, shape, dt=f32):
            return ctx.enter_context(nc.sbuf_tensor(name, shape, dt))

        def bank(name):
            return ctx.enter_context(nc.psum_tensor(name, [P, 512], f32))

        def sem(name):
            return ctx.enter_context(nc.semaphore(name))

        identity = sb("identity", [P, P])
        row_numbers = sb("row_numbers", [KP, KT])
        indices = sb("indices", [P, TILES, NUM_TABLES], i32)
        ids = [sb(f"ids{h}", [P, HALF, PAIR_SAMPLES], i32) for h in range(2)]
        rows = sb("rows", [P, 2, NT, P])
        table_hi = sb("table_hi", [KP, X, KT * P], f32r)
        table_lo = sb("table_lo", [KP, X, KT * P], f32r)
        onehot = sb("onehot", [KP, 2, KT, PAIR_SAMPLES], f32r)
        rows_t = sb("rows_t", [P, TILES, QUADS, 4, B])
        dots = sb("dots", [P, QUADS, FM])
        turned = sb("turned", [P, FM, B])
        pairs = sb("pairs", [P, PAIRS])
        pairs_t = sb("pairs_t", [P, len(ZC), GS])
        dense_t = sb("dense_t", [P, 2, GS])
        h1_t = sb("h1_t", [P, H1C, GS])
        h2_t = sb("h2_t", [P, H2C, GS])
        w1_sb = sb("w1_sb", [P, 1 + len(ZC), H1])
        w2_sb = sb("w2_sb", [P, H1C, H2])
        w3_sb = sb("w3_sb", [P, H2C])
        b1_sb = sb("b1_sb", [P, H1C])
        b2_sb = sb("b2_sb", [P, H2C])
        y_sb = h2_t[0:1, 0, :]
        w1_dense2 = pairs_t[:, 2, :]
        staged = [h1_t[0:KP, 0:2, :].rearrange("p c n -> p (c n)"),
                  h1_t[0:KP, 2:4, :].rearrange("p c n -> p (c n)"),
                  pairs_t[0:KP, 0:2, :].rearrange("p c n -> p (c n)")]
        STAGED = len(staged)

        transpose_banks = [bank(f"transpose_bank{i}") for i in range(2)]
        lookup_banks = [bank(f"lookup_bank{i}") for i in range(2)]
        dots_banks = [bank(f"dots_bank{i}") for i in range(2)]
        layer_banks = [bank(f"layer_bank{i}") for i in range(2)]

        identity_loaded = sem("identity_loaded")
        numbers_loaded = sem("numbers_loaded")
        weights_loaded = sem("weights_loaded")
        table_staged = [sem(f"table_staged{s}") for s in range(STAGED)]
        hi_made = sem("hi_made")
        lo_made = sem("lo_made")
        memory_cleared = sem("memory_cleared")
        dense_weights_summed = sem("dense_weights_summed")
        indices_loaded = [sem(f"indices_loaded{t}") for t in range(TILES)]
        ids_loaded = [sem(f"ids_loaded{h}") for h in range(2)]
        dense_loaded = [sem(f"dense_loaded{s}") for s in range(2)]
        gathers_begun = sem("gathers_begun")
        gathered = [[sem(f"gathered{s}_{b}") for b in range(NB)] for s in range(2)]
        onehot_made = sem("onehot_made")
        looked_up = sem("looked_up")
        lookup_stored = sem("lookup_stored")
        transposed = sem("transposed")
        transposed_stored = sem("transposed_stored")
        dense_stored = sem("dense_stored")
        dots_done = sem("dots_done")
        dots_stored_act = sem("dots_stored_act")
        dots_stored_dve = sem("dots_stored_dve")
        dots_turned = sem("dots_turned")
        pairs_packed = sem("pairs_packed")
        pairs_transposed = sem("pairs_transposed")
        pairs_t_stored = sem("pairs_t_stored")
        layer_done = sem("layer_done")
        layer_stored = sem("layer_stored")
        out_stored = sem("out_stored")

        def looked_up_before(g, t, k=0):
            return (g * 2 + t // 2) * X + (len(CHUNKS[0]) if t % 2 else 0) + k

        def lookup_slot(t, k):
            return looked_up_before(0, t, k) % 2

        def after(g, t):
            return (g, t + 1) if t + 1 < TILES else (g + 1, 0)

        FIRST_STEPS = [(0, 0), (0, 1), (0, 2)]
        LAST = (GROUPS - 1, TILES - 1)

        block = ctx.enter_context(nc.Block())

        @block.sync
        def _(sp):
            def load_indices(g, t):
                tile = g * TILES + t
                if counts(tile - 3):
                    sp.wait_ge(transposed, (tile - 3) * NB)
                sp.dma_start(indices[:, t, :], ids_tiles[bass.ds(tile, 1), :, :].rearrange("a p f -> p (a f)")
                             ).then_inc(indices_loaded[t], 16)

            def load_dense(g, t):
                tile = g * TILES + t
                if counts(tile - 1):
                    sp.wait_ge(transposed, (tile - 1) * NB)
                sp.dma_start(rows[:, t % 2, 0, :], dense[bass.ds(tile * P, P), :]
                             ).then_inc(dense_loaded[t % 2], 16)

            def load_ids(g, t, h):
                tables = CHUNKS[t % 2][h * HALF:(h + 1) * HALF]
                before = looked_up_before(g, t)
                made = before if h else before - len(CHUNKS[(t + 1) % 2]) + HALF
                if counts(made):
                    sp.wait_ge(onehot_made, made)
                sp.dma_start(ids[h][:, 0:len(tables), :],
                             ids_rows[tables[0]:tables[-1] + 1,
                                      bass.ds(g * GS + (t // 2) * PAIR_SAMPLES, PAIR_SAMPLES)]
                             .partition_broadcast(P)).then_inc(ids_loaded[h], 16)

            def load_tile(g, t):
                load_indices(g, t)
                load_ids(g, t, 0)
                load_ids(g, t, 1)
                load_dense(g, t)

            def stage_table(x):
                s = x % STAGED
                if x >= STAGED:
                    sp.wait_ge(lo_made, x - STAGED + 1)
                full = KP // 16 * 16
                src = looked_up_tables[x].rearrange("(p k) d -> p (k d)", k=KT)
                sp.dma_start(staged[s][0:full, :], src[0:full, :]).then_inc(table_staged[s], 16)
                sp.dma_start(staged[s][full:KP, :], src[full:KP, :]).then_inc(table_staged[s], 16)

            load_indices(0, 0)
            stage_table(0)
            load_ids(0, 0, 0)
            sp.dma_start(row_numbers[:], row_numbers_c).then_inc(numbers_loaded, 16)
            stage_table(1)
            sp.dma_start(identity[:], identity_c).then_inc(identity_loaded, 16)
            load_dense(0, 0)
            stage_table(2)
            load_ids(0, 0, 1)
            stage_table(3)
            stage_table(4)
            load_indices(0, 1)
            stage_table(5)
            stage_table(6)
            load_ids(0, 1, 0)
            load_dense(0, 1)
            sp.dma_start(w1_sb[:, 0, :], w1[0:P, :]).then_inc(weights_loaded, 16)
            sp.dma_start(w1_dense2, w1[P:2 * P, :]).then_inc(weights_loaded, 16)
            for c, (at, n) in enumerate(ZC):
                sp.dma_start(w1_sb[0:n, 1 + c, :], w1[2 * P + at:2 * P + at + n, :]).then_inc(weights_loaded, 16)
            sp.dma_start(w2_sb[:], w2.rearrange("(c p) n -> p c n", p=P)).then_inc(weights_loaded, 16)
            sp.dma_start(w3_sb[:], w3).then_inc(weights_loaded, 16)
            sp.dma_start(b1_sb[:], b1).then_inc(weights_loaded, 16)
            sp.dma_start(b2_sb[:], b2).then_inc(weights_loaded, 16)
            load_indices(0, 2)
            load_ids(0, 1, 1)
            load_ids(0, 2, 0)
            load_ids(0, 2, 1)
            load_dense(0, 2)
            load_tile(0, 3)
            with sp.Fori(1, GROUPS) as g:
                for t in range(TILES):
                    load_tile(g, t)

        WEIGHT_LOADS = 2 + len(ZC) + 4

        @block.gpsimd
        def _(pool):
            def gather_tile(g, t):
                tile = g * TILES + t
                pool.wait_ge(indices_loaded[t], (g + 1) * 16)
                if counts(tile - 1):
                    pool.wait_ge(transposed, (tile - 1) * NB)
                pool.sem_inc(gathers_begun, 1)
                for n, f in enumerate(GATHERED):
                    nc.gpsimd.indirect_dma_start(
                        rows[:, t % 2, 1 + n, :], None, gathered_tables[n],
                        bass.IndirectOffsetOnAxis(indices[:, t, f:f + 1], 0)
                    ).then_inc(gathered[t % 2][(1 + n) // TB], 16)

            for t in range(TILES):
                gather_tile(0, t)
            with pool.Fori(1, GROUPS) as g:
                for t in range(TILES):
                    gather_tile(g, t)

        @block.tensor
        def _(pe):
            def transpose_pairs(g, t, step):
                tile = g * TILES + t
                pe.wait_ge(pairs_packed, tile + 1)
                pe.wait_ge(transposed_stored, step * NB - 1)
                for c, (at, n) in enumerate(ZC):
                    last = nc.tensor.transpose(transpose_banks[0][0:n, c * P:(c + 1) * P],
                                               pairs[:, at:at + n], identity[:])
                last.then_inc(pairs_transposed, 1)

            def transpose_features(g, t, b):
                tile = g * TILES + t
                features = range(b * TB, (b + 1) * TB)
                if b == 0:
                    pe.wait_ge(dense_loaded[t % 2], (g * 2 + t // 2 + 1) * 16)
                    if counts(tile):
                        pe.wait_ge(transposed_stored, tile * NB)
                elif b == 1:
                    if counts(tile - 1):
                        pe.wait_ge(pairs_t_stored, tile - 1)
                else:
                    pe.wait_ge(transposed_stored, tile * NB + b - 1)
                pe.wait_ge(gathered[t % 2][b], (g * 2 + t // 2 + 1) * 16 * (TB - (b == 0)))
                into = transpose_banks[(b + 1) % 2]
                for i, f in enumerate(features):
                    last = nc.tensor.transpose(into[:, i * P:(i + 1) * P], rows[:, t % 2, f, :], identity[:])
                last.then_inc(transposed, 1)

            def look_up(g, t, k):
                x = CHUNKS[t % 2][k]
                before = looked_up_before(g, t, k)
                pe.wait_ge(onehot_made, before + 1)
                if counts(before - 1):
                    pe.wait_ge(lookup_stored, before - 1)
                s = lookup_slot(t, k)
                for n in range(KT):
                    for half in (table_hi, table_lo):
                        last = nc.tensor.matmul(lookup_banks[s][:, 0:PAIR_SAMPLES],
                                                half[:, x, n * P:(n + 1) * P], onehot[:, s, n, :],
                                                start=(n == 0 and half is table_hi),
                                                stop=(n == KT - 1 and half is table_lo))
                last.then_inc(looked_up, 1)

            def dot_products(g, t):
                tile = g * TILES + t
                pe.wait_ge(transposed_stored, (tile + 1) * NB)
                pe.wait_ge(lookup_stored, (g * 2 + t // 2 + 1) * X)
                for i in range(GB):
                    if counts(tile * GB + i - 1):
                        pe.wait_ge(dots_stored_act, tile * GB + i - 1)
                        pe.wait_ge(dots_stored_dve, tile * GB + i - 1)
                    for b in range(QB):
                        quad = rows_t[:, t, i * QB + b, :, :]
                        last = nc.tensor.matmul(dots_banks[i % 2][0:3 * B + FM, b * 4 * FM:(b + 1) * 4 * FM],
                                                quad.rearrange("p j f -> p (j f)")[:, 1:1 + 3 * B + FM],
                                                quad[:, :, 0:FM], start=True, stop=True)
                    last.then_inc(dots_done, 1)

            def step(g, t, look_ups=True):
                ahead = range(len(CHUNKS[(t + 1) % 2])) if look_ups else ()
                transpose_features(g, t, 0)
                transpose_features(g, t, 1)
                for k, batches in enumerate(((2, 3), (4,), (), ())):
                    if k in ahead:
                        look_up(*after(g, t), k)
                    for b in batches:
                        transpose_features(g, t, b)

            def layer_1(g, outputs, at=0, n=GS, banks_used=0):
                for m in outputs:
                    use = g * USES + banks_used + m
                    if m >= 2 or banks_used:
                        pe.wait_ge(layer_stored, use - 1)
                    into = layer_banks[(banks_used + m) % 2][:, 0:n]
                    nc.tensor.matmul(into, w1_sb[:, 0, m * P:(m + 1) * P],
                                     dense_t[:, bass.ds(g % 2, 1), at:at + n].rearrange("p g s -> p (g s)"),
                                     start=True, stop=False)
                    for c, (_, k) in enumerate(ZC):
                        last = nc.tensor.matmul(into, w1_sb[0:k, 1 + c, m * P:(m + 1) * P],
                                                pairs_t[0:k, c, at:at + n], start=False,
                                                stop=(c == len(ZC) - 1))
                    last.then_inc(layer_done, 1)

            def layer_2(g, at=0, n=GS, banks_used=0):
                pe.wait_ge(layer_stored, g * USES + banks_used + USE_L2)
                for m in range(H2C):
                    into = layer_banks[(banks_used + USE_L2 + m) % 2][:, 0:n]
                    for c in range(H1C):
                        last = nc.tensor.matmul(into, w2_sb[:, c, m * P:(m + 1) * P], h1_t[:, c, at:at + n],
                                                start=(c == 0), stop=(c == H1C - 1))
                    last.then_inc(layer_done, 1)

            def layer_3(g, at=0, n=GS, banks_used=0):
                pe.wait_ge(layer_stored, g * USES + banks_used + USE_L3)
                into = layer_banks[(banks_used + USE_L3) % 2]
                for c in range(H2C):
                    last = nc.tensor.matmul(into[0:1, 0:n], w3_sb[:, c:c + 1], h2_t[:, c, at:at + n],
                                            start=(c == 0), stop=(c == H2C - 1))
                last.then_inc(layer_done, 1)

            for k in range(len(CHUNKS[0])):
                pe.wait_ge(lo_made, k + 1)
                look_up(0, 0, k)
                if k == 0:
                    pe.wait_ge(identity_loaded, 16)
            pe.wait_ge(lo_made, X)
            step(0, 0)
            pe.wait_ge(memory_cleared, 2)
            dot_products(0, 0)
            step(0, 1)
            transpose_pairs(0, 0, 2)
            dot_products(0, 1)
            step(0, 2)
            pe.wait_ge(weights_loaded, WEIGHT_LOADS * 16)
            pe.wait_ge(dense_weights_summed, 1)
            with pe.Fori(0, GROUPS - 1) as g:
                T = g * TILES
                transpose_pairs(g, 1, T + 3)
                dot_products(g, 2)
                step(g, 3)
                transpose_pairs(g, 2, T + 4)
                dot_products(g, 3)
                step(g + 1, 0)
                transpose_pairs(g, 3, T + 5)
                dot_products(g + 1, 0)
                pe.wait_ge(pairs_t_stored, T + 4)
                pe.wait_ge(dense_stored, T + 4)
                layer_1(g, (0, 1))
                step(g + 1, 1)
                layer_1(g, (2, 3))
                transpose_pairs(g + 1, 0, T + 6)
                dot_products(g + 1, 1)
                layer_2(g)
                step(g + 1, 2)
                layer_3(g)
                pe.wait_ge(layer_stored, (g + 1) * USES)
            g, t = LAST
            transpose_pairs(g, 1, ALL_TILES - 1)
            dot_products(g, 2)
            step(g, t, look_ups=False)
            dot_products(g, t)
            transpose_pairs(g, 2, ALL_TILES)
            pe.wait_ge(pairs_t_stored, ALL_TILES - 1)
            pe.wait_ge(dense_stored, ALL_TILES)
            LAST_SAMPLES = (0, GS)
            transpose_banks.reverse()
            transpose_pairs(g, 3, ALL_TILES)
            transpose_banks.reverse()
            pe.wait_ge(pairs_t_stored, ALL_TILES)
            layer_1(g, range(H1C))
            layer_2(g)
            layer_3(g)

        ACT_BLOCKS = (0, 1, 2)
        DVE_BLOCKS = (3,)

        def dots_block(i, j):
            return dots_banks[i % 2][B * j:B * j + FM, 0:QB * 4 * FM].rearrange(
                "p (b j f) -> p b j f", j=4, f=FM)[:, :, j, :]

        @block.scalar
        def _(act):
            def store_look_up(g, t, k):
                s = lookup_slot(t, k)
                act.wait_ge(looked_up, looked_up_before(g, t, k) + 1)
                pair = rows_t[:, t - t % 2:t - t % 2 + 2, :, :, NT + CHUNKS[t % 2][k]]
                nc.scalar.copy(pair.rearrange("p a q j -> p a j q"),
                               lookup_banks[s][:, 0:PAIR_SAMPLES].rearrange("p (a j q) -> p a j q", a=2, j=4)
                               ).then_inc(lookup_stored, 1)

            def store_features(g, t, b):
                into = transpose_banks[(b + 1) % 2]
                act.wait_ge(transposed, (g * TILES + t) * NB + b + 1)
                if b == 0:
                    nc.scalar.copy(dense_t[:, bass.ds(g % 2, 1), t * P:(t + 1) * P].rearrange("p g s -> p (g s)"),
                                   into[:, 0:P]).then_inc(dense_stored, 1)
                nc.scalar.copy(rows_t[:, t, :, :, b * TB:(b + 1) * TB].rearrange("p q j f -> p f j q"),
                               into[:, :].rearrange("p (f j q) -> p f j q", f=TB, j=4)
                               ).then_inc(transposed_stored, 1)

            def step(g, t, look_ups=True):
                ahead = range(len(CHUNKS[(t + 1) % 2])) if look_ups else ()
                store_features(g, t, 0)
                store_features(g, t, 1)
                for k, batches in enumerate(((2, 3), (4,), (), ())):
                    if k in ahead:
                        store_look_up(*after(g, t), k)
                    for b in batches:
                        store_features(g, t, b)

            def store_dots(g, t):
                tile = g * TILES + t
                if counts(tile):
                    act.wait_ge(dots_turned, tile)
                for i in range(GB):
                    act.wait_ge(dots_done, tile * GB + i + 1)
                    for j in ACT_BLOCKS:
                        last = nc.scalar.copy(dots[B * j:B * j + FM, i * QB:(i + 1) * QB, :], dots_block(i, j))
                    last.then_inc(dots_stored_act, 1)

            def store_layer_1(g, outputs, at=0, n=GS, banks_used=0):
                for m in outputs:
                    act.wait_ge(layer_done, g * USES + banks_used + m + 1)
                    nc.scalar.activation(h1_t[:, m, at:at + n], layer_banks[(banks_used + m) % 2][:, 0:n], RELU,
                                         bias=b1_sb[:, m:m + 1]).then_inc(layer_stored, 1)

            def store_layer_2(g, at=0, n=GS, banks_used=0):
                for m in range(H2C):
                    act.wait_ge(layer_done, g * USES + banks_used + USE_L2 + m + 1)
                    nc.scalar.activation(h2_t[:, m, at:at + n],
                                         layer_banks[(banks_used + USE_L2 + m) % 2][:, 0:n], RELU,
                                         bias=b2_sb[:, m:m + 1]).then_inc(layer_stored, 1)

            def store_layer_3(g, at=0, n=GS, banks_used=0):
                act.wait_ge(layer_done, g * USES + banks_used + USES)
                nc.scalar.copy(y_sb[:, at:at + n], layer_banks[(banks_used + USE_L3) % 2][0:1, 0:n]
                               ).then_inc(layer_stored, 1)
                act.wait_ge(layer_stored, g * USES + banks_used + USES)
                act.dma_start(out[0:1, bass.ds(g * GS + at, n)], y_sb[:, at:at + n]).then_inc(out_stored, 16)

            for x in range(X):
                act.wait_ge(table_staged[x % STAGED], (x // STAGED + 1) * 32)
                nc.scalar.copy(table_hi[:, x, :], staged[x % STAGED]).then_inc(hi_made, 1)
            for k in range(len(CHUNKS[0])):
                store_look_up(0, 0, k)
            step(0, 0)
            act.wait_ge(memory_cleared, 2)
            store_dots(0, 0)
            step(0, 1)
            store_dots(0, 1)
            step(0, 2)
            act.wait_ge(weights_loaded, WEIGHT_LOADS * 16)
            with act.Fori(0, GROUPS - 1) as g:
                store_dots(g, 2)
                step(g, 3)
                store_dots(g, 3)
                step(g + 1, 0)
                store_dots(g + 1, 0)
                store_layer_1(g, (0, 1))
                step(g + 1, 1)
                store_layer_1(g, (2, 3))
                store_dots(g + 1, 1)
                store_layer_2(g)
                step(g + 1, 2)
                store_layer_3(g)
                act.wait_ge(out_stored, (g + 1) * 16)
            g, t = LAST
            store_dots(g, 2)
            step(g, t, look_ups=False)
            store_dots(g, t)
            store_layer_1(g, range(H1C))
            store_layer_2(g)
            store_layer_3(g)
            act.wait_ge(out_stored, GROUPS * 16)

        @block.vector
        def _(dve):
            def start_onehot(g, t, k):
                h = k // HALF
                before = looked_up_before(g, t, k)
                dve.wait_ge(ids_loaded[h], (g * TILES + t + 1) * 16)
                if counts(before - 1):
                    dve.wait_ge(looked_up, before - 1)

            def make_onehot(t, k, n):
                return nc.vector.tensor_scalar(onehot[:, lookup_slot(t, k), n, :],
                                               ids[k // HALF][0:KP, k % HALF, :],
                                               row_numbers[:, n:n + 1], None, ALU.is_equal)

            def whole_onehot(g, t, k):
                start_onehot(g, t, k)
                for n in range(KT):
                    last = make_onehot(t, k, n)
                last.then_inc(onehot_made, 1)

            def store_dots(g, t, i):
                tile = g * TILES + t
                dve.wait_ge(dots_done, tile * GB + i + 1)
                for j in DVE_BLOCKS:
                    last = nc.vector.tensor_copy(dots[B * j:B * j + FM, i * QB:(i + 1) * QB, :], dots_block(i, j))
                last.then_inc(dots_stored_dve, 1)

            def pack_pairs(g, t):
                tile = g * TILES + t
                dve.wait_ge(dots_stored_act, (tile + 1) * GB)
                dve.wait_ge(dots_stored_dve, (tile + 1) * GB)
                nc.vector.transpose(turned[:, :, :], dots[:, :, :].rearrange("p q i -> p i q")
                                    ).then_inc(dots_turned, 1)
                dve.wait_ge(dots_turned, tile + 1)
                if counts(tile):
                    dve.wait_ge(pairs_transposed, tile)
                for i in range(FM):
                    last = nc.vector.tensor_copy(pairs[:, PAIR_AT[i]:PAIR_AT[i + 1]], turned[:, i, i:FM])
                last.then_inc(pairs_packed, 1)

            def store_pairs_t(g, t, banks=transpose_banks):
                tile = g * TILES + t
                dve.wait_ge(pairs_transposed, tile + 1)
                for c in range(0, len(ZC), 2):
                    n = ZC[c][1]
                    cs = min(2, len(ZC) - c)
                    last = nc.vector.tensor_copy(
                        pairs_t[0:n, c:c + cs, t * P:(t + 1) * P],
                        banks[0][0:n, c * P:(c + cs) * P].rearrange("p (c s) -> p c s", c=cs))
                last.then_inc(pairs_t_stored, 1)

            def step(g, t, dots_of, look_ups=True):
                ahead = after(g, t)
                if look_ups:
                    start_onehot(*ahead, 0)
                for i in range(GB):
                    store_dots(*dots_of, i)
                    if look_ups:
                        if i == GB // 2:
                            start_onehot(*ahead, 1)
                        for n in range(2):
                            j = (2 * i + n) % KT
                            last = make_onehot(ahead[1], (2 * i + n) // KT, j)
                            if j == KT - 1:
                                last.then_inc(onehot_made, 1)
                pack_pairs(*dots_of)
                if look_ups:
                    for k in range(2, len(CHUNKS[(t + 1) % 2])):
                        whole_onehot(*ahead, k)

            nc.vector.memset(dots[:], 0.0).then_inc(memory_cleared, 1)
            nc.vector.memset(rows_t[:, :, :, :, F:B], 0.0).then_inc(memory_cleared, 1)
            dve.wait_ge(numbers_loaded, 16)

            def make_lo(x):
                dve.wait_ge(table_staged[x % STAGED], (x // STAGED + 1) * 32)
                dve.wait_ge(hi_made, x + 1)
                nc.vector.tensor_tensor(table_lo[:, x, :], staged[x % STAGED], table_hi[:, x, :].bitcast(f32),
                                        ALU.subtract).then_inc(lo_made, 1)

            for x in range(X):
                make_lo(x)
                if x < len(CHUNKS[0]):
                    whole_onehot(0, 0, x)
            for k in range(len(CHUNKS[1])):
                whole_onehot(0, 1, k)
            dve.wait_ge(weights_loaded, WEIGHT_LOADS * 16)
            nc.vector.tensor_tensor(w1_sb[:, 0, :], w1_sb[:, 0, :], w1_dense2, ALU.add
                                    ).then_inc(dense_weights_summed, 1)
            step(0, 1, (0, 0))
            store_pairs_t(0, 0)
            step(0, 2, (0, 1))
            with dve.Fori(0, GROUPS - 1) as g:
                store_pairs_t(g, 1)
                step(g, 3, (g, 2))
                store_pairs_t(g, 2)
                step(g + 1, 0, (g, 3))
                store_pairs_t(g, 3)
                step(g + 1, 1, (g + 1, 0))
                store_pairs_t(g + 1, 0)
                step(g + 1, 2, (g + 1, 1))
            g, t = LAST
            store_pairs_t(g, 1)
            step(g, t, (g, 2), look_ups=False)
            for i in range(GB):
                store_dots(g, t, i)
            store_pairs_t(g, 2)
            pack_pairs(g, t)
            store_pairs_t(g, t, banks=transpose_banks[::-1])


def kernel(**inputs):
    import numpy as np
    import concourse.bacc as bacc
    from concourse.bass_utils import run_bass_kernel_spmd

    def pair_row(i, j):
        a, b = sorted((ORDER[i], ORDER[j]))
        return P + a * (F - 1) - a * (a - 1) // 2 + b - a - 1

    w1_rows = list(range(P)) + list(range(P + PAIRS, P + PAIRS + P))
    w1_rows += [pair_row(i, j) for i in range(F) for j in range(i + 1, F)]
    ids = np.asarray(inputs["ids"])
    arrays = {
        "dense": np.asarray(inputs["r_dense_features"]),
        "ids_tiles": ids.reshape(BATCH // P, P, NUM_TABLES),
        "ids_rows": ids.T[list(LOOKED_UP)],
        "w1": np.asarray(inputs["W_top1"])[w1_rows],
        "b1": np.asarray(inputs["b_top1"]).reshape(H1C, P).T,
        "w2": np.asarray(inputs["W_top2"]),
        "b2": np.asarray(inputs["b_top2"]).reshape(H2C, P).T,
        "w3": np.asarray(inputs["W_top3"]).reshape(H2C, P).T,
        "identity": np.eye(P, dtype=np.float32),
        "row_numbers": np.arange(ROWS, dtype=np.float32).reshape(KP, KT),
    }
    for f in range(NUM_TABLES):
        arrays[f"tbl_{f}"] = np.asarray(inputs[f"tbl_{f}"])
    arrays = {f"in_{k}": np.ascontiguousarray(a) for k, a in arrays.items()}

    nc = bacc.Bacc("TRN2", target_bir_lowering=False, num_devices=1)
    ap = {k[3:]: nc.dram_tensor(k, a.shape, mybir.dt.from_np(a.dtype), kind="ExternalInput").ap()
          for k, a in arrays.items()}
    out = nc.dram_tensor("out", [1, BATCH], mybir.dt.float32, kind="ExternalOutput").ap()
    dlrm_kernel(nc, ap["dense"], ap["ids_tiles"], ap["ids_rows"], [ap[f"tbl_{f}"] for f in GATHERED],
                [ap[f"tbl_{f}"] for f in LOOKED_UP], ap["w1"], ap["b1"], ap["w2"], ap["b2"], ap["w3"],
                ap["identity"], ap["row_numbers"], out)
    result = run_bass_kernel_spmd(nc, [arrays], core_ids=[0])
    return result.results[0]["out"].reshape(BATCH, 1)
```

```python
import concourse.bass as bass
from concourse import mybir
from contextlib import ExitStack

BATCH = 2048
P = 128
NUM_TABLES = 26
F = NUM_TABLES + 1
FM = F - 1
PAIRS = F * FM // 2
LOOKED_UP = (2, 4, 5, 6, 10, 23, 24)
MIXED = LOOKED_UP[0]
GATHERED = tuple(f for f in range(NUM_TABLES) if f not in LOOKED_UP) + (MIXED,)
ORDER = (0,) + tuple(1 + f for f in GATHERED + LOOKED_UP[1:])
X = len(LOOKED_UP)
NG = len(GATHERED)
ROWS = 1000
KT = 8
KP = ROWS // KT
B = 32

TILES = 4
GROUPS = BATCH // (P * TILES)
ALL_TILES = GROUPS * TILES
GS = P * TILES
QUADS = P // 4
DUO_SAMPLES = 2 * P
FULL_CHUNKS = ((0, 1, 2, 3), (4, 5, 6))
CHUNKS = ((1, 2, 3), (4, 5, 6))
HALF = 2
TB = 4
NB = NG // TB
QB = 4
GB = QUADS // QB
ZC = [(c, min(P, PAIRS - c)) for c in range(0, PAIRS, P)]
PAIR_AT = [sum(FM - k for k in range(i)) for i in range(F)]
H1, H2 = 512, 256
H1C, H2C = H1 // P, H2 // P
USE_DENSE = H1C
USES = H1C + 1 + H2C + 1
assert USES % 2 == 0 and NG % TB == 0 and NB % 2 == 1


def counts(value):
    return not isinstance(value, int) or value > 0


def dlrm_kernel(nc, dense, ids_tiles, ids_rows, gathered_tables, looked_up_tables, w1, b1, w2, b2, w3,
                identity_c, row_numbers_c, out):
    f32 = mybir.dt.float32
    f32r = mybir.dt.float32r
    i32 = mybir.dt.int32
    ALU = mybir.AluOpType
    RELU = mybir.ActivationFunctionType.Relu

    ctx = ExitStack()
    with ctx:
        def sb(name, shape, dt=f32):
            return ctx.enter_context(nc.sbuf_tensor(name, shape, dt))

        def bank(name):
            return ctx.enter_context(nc.psum_tensor(name, [P, 512], f32))

        def sem(name):
            return ctx.enter_context(nc.semaphore(name))

        identity = sb("identity", [P, P])
        row_numbers = sb("row_numbers", [KP, KT])
        indices = sb("indices", [P, TILES, NUM_TABLES], i32)
        ids = [sb(f"ids{h}", [P, HALF, DUO_SAMPLES], i32) for h in range(2)]
        rows = sb("rows", [P, 2, NG, P])
        dense_rows = sb("dense_rows", [P, 2, P])
        table_hi = sb("table_hi", [KP, X, KT * P], f32r)
        table_lo = sb("table_lo", [KP, X, KT * P], f32r)
        onehot = sb("onehot", [KP, 2, KT, DUO_SAMPLES], f32r)
        rows_t = sb("rows_t", [P, TILES, QUADS, 4, B])
        dots = sb("dots", [P, QUADS, FM])
        turned = sb("turned", [P, FM, B])
        pairs = sb("pairs", [P, PAIRS])
        pairs_t = sb("pairs_t", [P, len(ZC), GS])
        dense_t = sb("dense_t", [P, GS])
        h1_t = sb("h1_t", [P, H1C, GS])
        h2_t = sb("h2_t", [P, H2C, GS])
        w1_sb = sb("w1_sb", [P, 1 + len(ZC), H1])
        w2_sb = sb("w2_sb", [P, H1C, H2])
        w3_sb = sb("w3_sb", [P, H2C])
        b1_sb = sb("b1_sb", [P, H1C])
        b2_sb = sb("b2_sb", [P, H2C])
        y_sb = sb("y_sb", [P, ALL_TILES])
        w1_dense2 = pairs_t[:, 2, :]
        staged = [h1_t[0:KP, 0:2, :].rearrange("p c n -> p (c n)"),
                  h1_t[0:KP, 2:4, :].rearrange("p c n -> p (c n)"),
                  pairs_t[0:KP, 0:2, :].rearrange("p c n -> p (c n)")]
        STAGED = len(staged)

        transpose_banks = [bank(f"transpose_bank{i}") for i in range(2)]
        lookup_banks = [bank(f"lookup_bank{i}") for i in range(2)]
        dots_banks = [bank(f"dots_bank{i}") for i in range(2)]
        layer_banks = [bank(f"layer_bank{i}") for i in range(2)]

        identity_loaded = sem("identity_loaded")
        numbers_loaded = sem("numbers_loaded")
        weights_loaded = sem("weights_loaded")
        table_staged = [sem(f"table_staged{s}") for s in range(STAGED)]
        hi_made = sem("hi_made")
        lo_made = sem("lo_made")
        memory_cleared = sem("memory_cleared")
        dense_weights_summed = sem("dense_weights_summed")
        indices_loaded = [sem(f"indices_loaded{t}") for t in range(TILES)]
        ids_loaded = [sem(f"ids_loaded{h}") for h in range(2)]
        dense_loaded = sem("dense_loaded")
        gathers_begun = sem("gathers_begun")
        gathered = [[sem(f"gathered{s}_{b}") for b in range(NB)] for s in range(2)]
        onehot_made = sem("onehot_made")
        looked_up = sem("looked_up")
        lookup_stored = sem("lookup_stored")
        transposed = sem("transposed")
        transposed_stored = sem("transposed_stored")
        dense_stored = sem("dense_stored")
        dots_done = sem("dots_done")
        dots_stored_act = sem("dots_stored_act")
        dots_stored_dve = sem("dots_stored_dve")
        dots_turned = sem("dots_turned")
        pairs_packed = sem("pairs_packed")
        pairs_transposed = sem("pairs_transposed")
        pairs_t_stored = sem("pairs_t_stored")
        layer_done = sem("layer_done")
        layer_stored = sem("layer_stored")
        out_stored = sem("out_stored")

        def first_group(g):
            return isinstance(g, int) and g == 0

        def mixed_looked_up(g, t):
            return first_group(g) or t >= 2

        def chunk(g, t):
            return (FULL_CHUNKS if mixed_looked_up(g, t) else CHUNKS)[t % 2]

        def looked_up_before(g, t, k=0):
            before = t // 2 * X if first_group(g) else g * (2 * X - 1) + 1 + t // 2 * (X - 1)
            return before + (len(chunk(g, t - 1)) if t % 2 else 0) + k

        def lookup_slot(g, t, k):
            return looked_up_before(0 if first_group(g) else 1, t, k) % 2

        def lookup_freed(g, t, k):
            return looked_up_before(g, t, k) - (1 if t or k else 0)

        def batch_size(g, t, b):
            return TB - (b == NB - 1 and mixed_looked_up(g, t))

        def batch_gathered(g, t, b):
            extra = g if b == NB - 1 else 0
            return ((g * 2 + t // 2 + 1) * (TB - (b == NB - 1)) + extra) * 16

        def uses_before(g, t):
            return 2 + (g * 2 + t // 2) * USES

        def layer_2_use(shift, between):
            return shift + H1C + between

        def layer_3_use(shift, between, late):
            return layer_2_use(shift, between) + H2C + late

        WHOLE = dict(n=DUO_SAMPLES, shift=0, between=1, late=0)
        LAST_DUO_BUT_ONE = dict(WHOLE, between=0, late=H1C)
        LAST_TILE_BUT_ONE = dict(n=P, shift=-2, between=1, late=H1C)
        LAST_TILE = dict(n=P, shift=layer_3_use(-2, 1, 0), between=1, late=0)
        LAST_USE = layer_3_use(LAST_TILE["shift"], 1, 0)

        def after(g, t):
            return (g, t + 1) if t + 1 < TILES else (g + 1, 0)

        BESIDE = ((2,), (3,), (4,), ())
        LAST = (GROUPS - 1, TILES - 1)

        block = ctx.enter_context(nc.Block())

        @block.sync
        def _(sp):
            def load_indices(g, t):
                tile = g * TILES + t
                if counts(tile - 3):
                    sp.wait_ge(transposed, (tile - 3) * NB)
                sp.dma_start(indices[:, t, :], ids_tiles[bass.ds(tile, 1), :, :].rearrange("a p f -> p (a f)")
                             ).then_inc(indices_loaded[t], 16)

            def load_dense(g, t):
                duo = g * 2 + t // 2
                if counts(duo):
                    sp.wait_ge(dense_stored, duo)
                sp.dma_start(dense_rows[:],
                             dense[bass.ds(duo * DUO_SAMPLES, DUO_SAMPLES), :].rearrange("(t p) d -> p t d", p=P)
                             ).then_inc(dense_loaded, 16)

            def load_ids(g, t, h):
                tables = chunk(g, t)[h * HALF:(h + 1) * HALF]
                before = looked_up_before(g, t)
                made = before if h else before - len(chunk(g, t - 1 if t else TILES - 1)) + HALF
                if counts(made):
                    sp.wait_ge(onehot_made, made)
                sp.dma_start(ids[h][:, 0:len(tables), :],
                             ids_rows[tables[0]:tables[-1] + 1,
                                      bass.ds(g * GS + (t // 2) * DUO_SAMPLES, DUO_SAMPLES)]
                             .partition_broadcast(P)).then_inc(ids_loaded[h], 16)

            def load_tile(g, t):
                load_indices(g, t)
                load_ids(g, t, 0)
                load_ids(g, t, 1)

            def stage_table(x):
                s = x % STAGED
                if x >= STAGED:
                    sp.wait_ge(lo_made, x - STAGED + 1)
                full = KP // 16 * 16
                src = looked_up_tables[x].rearrange("(p k) d -> p (k d)", k=KT)
                sp.dma_start(staged[s][0:full, :], src[0:full, :]).then_inc(table_staged[s], 16)
                sp.dma_start(staged[s][full:KP, :], src[full:KP, :]).then_inc(table_staged[s], 16)

            load_indices(0, 0)
            stage_table(0)
            load_ids(0, 0, 0)
            sp.dma_start(row_numbers[:], row_numbers_c).then_inc(numbers_loaded, 16)
            stage_table(1)
            sp.dma_start(identity[:], identity_c).then_inc(identity_loaded, 16)
            load_dense(0, 0)
            stage_table(2)
            load_ids(0, 0, 1)
            stage_table(3)
            stage_table(4)
            load_indices(0, 1)
            for x in range(5, X):
                stage_table(x)
            load_ids(0, 1, 0)
            sp.dma_start(w1_sb[:, 0, :], w1[0:P, :]).then_inc(weights_loaded, 16)
            sp.dma_start(w1_dense2, w1[P:2 * P, :]).then_inc(weights_loaded, 16)
            for c, (at, n) in enumerate(ZC):
                sp.dma_start(w1_sb[0:n, 1 + c, :], w1[2 * P + at:2 * P + at + n, :]).then_inc(weights_loaded, 16)
            sp.dma_start(w2_sb[:], w2.rearrange("(c p) n -> p c n", p=P)).then_inc(weights_loaded, 16)
            sp.dma_start(w3_sb[:], w3).then_inc(weights_loaded, 16)
            sp.dma_start(b1_sb[:], b1).then_inc(weights_loaded, 16)
            sp.dma_start(b2_sb[:], b2).then_inc(weights_loaded, 16)
            load_indices(0, 2)
            load_ids(0, 1, 1)
            load_ids(0, 2, 0)
            load_ids(0, 2, 1)
            load_dense(0, 2)
            load_tile(0, 3)
            with sp.Fori(1, GROUPS) as g:
                for t in range(TILES):
                    load_tile(g, t)
                    if t % 2 == 0:
                        load_dense(g, t)

        WEIGHT_LOADS = 2 + len(ZC) + 4

        @block.gpsimd
        def _(pool):
            def gather_tile(g, t):
                tile = g * TILES + t
                pool.wait_ge(indices_loaded[t], (g + 1) * 16)
                if counts(tile - 1):
                    pool.wait_ge(transposed, (tile - 1) * NB)
                pool.sem_inc(gathers_begun, 1)
                for n, f in enumerate(GATHERED[:-1] if mixed_looked_up(g, t) else GATHERED):
                    nc.gpsimd.indirect_dma_start(
                        rows[:, t % 2, n, :], None, gathered_tables[n],
                        bass.IndirectOffsetOnAxis(indices[:, t, f:f + 1], 0)
                    ).then_inc(gathered[t % 2][n // TB], 16)

            for t in range(TILES):
                gather_tile(0, t)
            with pool.Fori(1, GROUPS) as g:
                for t in range(TILES):
                    gather_tile(g, t)

        @block.tensor
        def _(pe):
            def transpose_pairs(g, t, stored, bank=0):
                tile = g * TILES + t
                pe.wait_ge(pairs_packed, tile + 1)
                pe.wait_ge(transposed_stored, stored)
                for c, (at, n) in enumerate(ZC):
                    last = nc.tensor.transpose(transpose_banks[bank][0:n, c * P:(c + 1) * P],
                                               pairs[:, at:at + n], identity[:])
                last.then_inc(pairs_transposed, 1)

            def transpose_features(g, t, b, bank=None):
                tile = g * TILES + t
                if b == 0:
                    if counts(tile):
                        pe.wait_ge(transposed_stored, tile * NB)
                elif b == 1:
                    if counts(tile - 1):
                        pe.wait_ge(pairs_t_stored, tile - 1)
                else:
                    pe.wait_ge(transposed_stored, tile * NB + b - (bank is None))
                pe.wait_ge(gathered[t % 2][b], batch_gathered(g, t, b))
                into = transpose_banks[(b + 1) % 2 if bank is None else bank]
                for i in range(batch_size(g, t, b)):
                    last = nc.tensor.transpose(into[:, i * P:(i + 1) * P], rows[:, t % 2, b * TB + i, :],
                                               identity[:])
                last.then_inc(transposed, 1)

            def transpose_dense(duo, bank):
                pe.wait_ge(dense_loaded, (duo + 1) * 16)
                for t in range(2):
                    last = nc.tensor.transpose(layer_banks[bank][:, t * P:(t + 1) * P], dense_rows[:, t, :],
                                               identity[:])
                last.then_inc(layer_done, 1)

            def look_up(g, t, k):
                x = chunk(g, t)[k]
                before = looked_up_before(g, t, k)
                pe.wait_ge(onehot_made, before + 1)
                if counts(lookup_freed(g, t, k)):
                    pe.wait_ge(lookup_stored, lookup_freed(g, t, k))
                s = lookup_slot(g, t, k)
                if isinstance(before, int) and before < X:
                    pe.wait_ge(lo_made, x + 1)
                for n in range(KT):
                    for half in (table_hi, table_lo):
                        last = nc.tensor.matmul(lookup_banks[s][:, 0:DUO_SAMPLES],
                                                half[:, x, n * P:(n + 1) * P], onehot[:, s, n, :],
                                                start=(n == 0 and half is table_hi),
                                                stop=(n == KT - 1 and half is table_lo))
                last.then_inc(looked_up, 1)

            def dot_products(g, t):
                tile = g * TILES + t
                pe.wait_ge(transposed_stored, (tile + 1) * NB)
                pe.wait_ge(dense_stored, g * 2 + t // 2 + 1)
                pe.wait_ge(lookup_stored, looked_up_before(g, t | 1, len(chunk(g, 1))))
                for i in range(GB):
                    if counts(tile * GB + i - 1):
                        pe.wait_ge(dots_stored_act, tile * GB + i - 1)
                        pe.wait_ge(dots_stored_dve, tile * GB + i - 1)
                    for b in range(QB):
                        quad = rows_t[:, t, i * QB + b, :, :]
                        last = nc.tensor.matmul(dots_banks[i % 2][0:3 * B + FM, b * 4 * FM:(b + 1) * 4 * FM],
                                                quad.rearrange("p j f -> p (j f)")[:, 1:1 + 3 * B + FM],
                                                quad[:, :, 0:FM], start=True, stop=True)
                    last.then_inc(dots_done, 1)

            def step(g, t):
                transpose_features(g, t, 0)
                transpose_features(g, t, 1)
                for k in range(len(chunk(*after(g, t)))):
                    look_up(*after(g, t), k)
                    for b in BESIDE[k]:
                        transpose_features(g, t, b)

            def layer_1(g, t, outputs, n, shift, between, late):
                before, at = uses_before(g, t), t * P
                for m in outputs:
                    pe.wait_ge(layer_stored, before + shift + m - 1)
                    into = layer_banks[(shift + m) % 2][:, 0:n]
                    nc.tensor.matmul(into, w1_sb[:, 0, m * P:(m + 1) * P], dense_t[:, at:at + n],
                                     start=True, stop=False)
                    for c, (_, k) in enumerate(ZC):
                        last = nc.tensor.matmul(into, w1_sb[0:k, 1 + c, m * P:(m + 1) * P],
                                                pairs_t[0:k, c, at:at + n], start=False,
                                                stop=(c == len(ZC) - 1))
                    last.then_inc(layer_done, 1)

            def layer_2(g, t, n, shift, between, late, outputs=range(H2C)):
                before, first, at = uses_before(g, t), layer_2_use(shift, between), t * P
                if outputs[0] == 0:
                    pe.wait_ge(layer_stored, before + shift + H1C)
                for m in outputs:
                    pe.wait_ge(layer_stored, before + first + m - 1)
                    into = layer_banks[(first + m) % 2][:, 0:n]
                    for c in range(H1C):
                        last = nc.tensor.matmul(into, w2_sb[:, c, m * P:(m + 1) * P], h1_t[:, c, at:at + n],
                                                start=(c == 0), stop=(c == H1C - 1))
                    last.then_inc(layer_done, 1)

            def layer_3(g, t, n, shift, between, late):
                use, at = layer_3_use(shift, between, late), t * P
                pe.wait_ge(layer_stored, uses_before(g, t) + use - (1 if late else 0))
                for a in range(n // P):
                    for c in range(H2C):
                        last = nc.tensor.matmul(layer_banks[use % 2][:, a:a + 1],
                                                h2_t[:, c, at + a * P:at + (a + 1) * P],
                                                w3_sb[:, c:c + 1], start=(c == 0), stop=(c == H2C - 1))
                last.then_inc(layer_done, 1)

            def next_dense(g, t):
                pe.wait_ge(layer_stored, uses_before(g, t) + USE_DENSE - 1)
                transpose_dense(g * 2 + t // 2 + 2, USE_DENSE % 2)

            for k in range(len(FULL_CHUNKS[0])):
                look_up(0, 0, k)
            pe.wait_ge(identity_loaded, 16)
            transpose_dense(0, 0)
            step(0, 0)
            pe.wait_ge(memory_cleared, 2)
            dot_products(0, 0)
            step(0, 1)
            transpose_pairs(0, 0, 2 * NB - 1)
            dot_products(0, 1)
            transpose_dense(1, 1)
            step(0, 2)
            pe.wait_ge(weights_loaded, WEIGHT_LOADS * 16)
            pe.wait_ge(dense_weights_summed, 1)
            with pe.Fori(0, GROUPS - 1) as g:
                T = g * TILES
                transpose_pairs(g, 1, (T + 3) * NB - 1)
                dot_products(g, 2)
                pe.wait_ge(pairs_t_stored, T + 2)
                layer_1(g, 0, range(H1C - 1), **WHOLE)
                step(g, 3)
                layer_1(g, 0, (H1C - 1,), **WHOLE)
                transpose_pairs(g, 2, (T + 4) * NB - 1)
                dot_products(g, 3)
                next_dense(g, 0)
                layer_2(g, 0, **WHOLE)
                step(g + 1, 0)
                layer_3(g, 0, **WHOLE)
                transpose_pairs(g, 3, (T + 5) * NB - 1)
                dot_products(g + 1, 0)
                pe.wait_ge(pairs_t_stored, T + 4)
                layer_1(g, 2, range(H1C - 1), **WHOLE)
                step(g + 1, 1)
                layer_1(g, 2, (H1C - 1,), **WHOLE)
                transpose_pairs(g + 1, 0, (T + 6) * NB - 1)
                dot_products(g + 1, 1)
                next_dense(g, 2)
                layer_2(g, 2, **WHOLE)
                step(g + 1, 2)
                layer_3(g, 2, **WHOLE)
            g, t = LAST
            batches_before = (ALL_TILES - 1) * NB
            transpose_pairs(g, 1, batches_before - 1)
            dot_products(g, 2)
            transpose_features(g, t, 0)
            transpose_features(g, t, 1)
            pe.wait_ge(pairs_t_stored, ALL_TILES - 2)
            layer_1(g, 0, range(H1C), **LAST_DUO_BUT_ONE)
            transpose_features(g, t, 2)
            transpose_features(g, t, 3)
            transpose_pairs(g, 2, batches_before + NB - 2, bank=1)
            layer_2(g, 0, **LAST_DUO_BUT_ONE)
            transpose_features(g, t, NB - 1, bank=0)
            pe.wait_ge(pairs_t_stored, ALL_TILES - 1)
            layer_1(g, 2, (0, 1), **LAST_TILE_BUT_ONE)
            dot_products(g, t)
            layer_1(g, 2, (2, 3), **LAST_TILE_BUT_ONE)
            layer_3(g, 0, **LAST_DUO_BUT_ONE)
            layer_2(g, 2, **LAST_TILE_BUT_ONE, outputs=(0,))
            transpose_pairs(g, t, ALL_TILES * NB, bank=1)
            layer_2(g, 2, **LAST_TILE_BUT_ONE, outputs=(1,))
            pe.wait_ge(pairs_t_stored, ALL_TILES)
            layer_1(g, t, range(H1C), **LAST_TILE)
            layer_3(g, 2, **LAST_TILE_BUT_ONE)
            layer_2(g, t, **LAST_TILE)
            layer_3(g, t, **LAST_TILE)

        ACT_BLOCKS = (0, 1)
        DVE_BLOCKS = (2, 3)

        def dots_block(i, j):
            return dots_banks[i % 2][B * j:B * j + FM, 0:QB * 4 * FM].rearrange(
                "p (b j f) -> p b j f", j=4, f=FM)[:, :, j, :]

        @block.scalar
        def _(act):
            def store_look_up(g, t, k):
                s = lookup_slot(g, t, k)
                act.wait_ge(looked_up, looked_up_before(g, t, k) + 1)
                pair = rows_t[:, t - t % 2:t - t % 2 + 2, :, :, NG + chunk(g, t)[k]]
                nc.scalar.copy(pair.rearrange("p a q j -> p a j q"),
                               lookup_banks[s][:, 0:DUO_SAMPLES].rearrange("p (a j q) -> p a j q", a=2, j=4)
                               ).then_inc(lookup_stored, 1)

            def store_features(g, t, b, bank=None):
                into = transpose_banks[(b + 1) % 2 if bank is None else bank]
                act.wait_ge(transposed, (g * TILES + t) * NB + b + 1)
                at, n = 1 + b * TB, batch_size(g, t, b)
                nc.scalar.copy(rows_t[:, t, :, :, at:at + n].rearrange("p q j f -> p f j q"),
                               into[:, 0:n * P].rearrange("p (f j q) -> p f j q", f=n, j=4)
                               ).then_inc(transposed_stored, 1)

            def store_dense(t, use, bank):
                act.wait_ge(layer_done, use + 1)
                src = layer_banks[bank][:, 0:DUO_SAMPLES]
                nc.scalar.copy(rows_t[:, t:t + 2, :, :, 0].rearrange("p t q j -> p t j q"),
                               src.rearrange("p (t j q) -> p t j q", t=2, j=4)).then_inc(dense_stored, 1)
                nc.scalar.copy(dense_t[:, t * P:t * P + DUO_SAMPLES], src).then_inc(layer_stored, 1)

            def step(g, t):
                store_features(g, t, 0)
                store_features(g, t, 1)
                for k in range(len(chunk(*after(g, t)))):
                    store_look_up(*after(g, t), k)
                    for b in BESIDE[k]:
                        store_features(g, t, b)

            def store_dots(g, t):
                tile = g * TILES + t
                if counts(tile):
                    act.wait_ge(dots_turned, tile)
                for i in range(GB):
                    act.wait_ge(dots_done, tile * GB + i + 1)
                    for j in ACT_BLOCKS:
                        last = nc.scalar.copy(dots[B * j:B * j + FM, i * QB:(i + 1) * QB, :], dots_block(i, j))
                    last.then_inc(dots_stored_act, 1)

            def store_layer_1(g, t, outputs, n, shift, between, late):
                before, at = uses_before(g, t), t * P
                for m in outputs:
                    act.wait_ge(layer_done, before + shift + m + 1)
                    nc.scalar.activation(h1_t[:, m, at:at + n], layer_banks[(shift + m) % 2][:, 0:n], RELU,
                                         bias=b1_sb[:, m:m + 1]).then_inc(layer_stored, 1)

            def store_layer_2(g, t, n, shift, between, late):
                before, first, at = uses_before(g, t), layer_2_use(shift, between), t * P
                for m in range(H2C):
                    act.wait_ge(layer_done, before + first + m + 1)
                    nc.scalar.activation(h2_t[:, m, at:at + n], layer_banks[(first + m) % 2][:, 0:n],
                                         RELU, bias=b2_sb[:, m:m + 1]).then_inc(layer_stored, 1)

            def store_layer_3(g, t, n, shift, between, late):
                use, tiles = layer_3_use(shift, between, late), n // P
                act.wait_ge(layer_done, uses_before(g, t) + use + 1)
                nc.scalar.copy(y_sb[:, bass.ds(g * TILES + t, tiles)], layer_banks[use % 2][:, 0:tiles]
                               ).then_inc(layer_stored, 1)

            def store_next_dense(g, t):
                store_dense(t, uses_before(g, t) + USE_DENSE, USE_DENSE % 2)

            for x in range(X):
                act.wait_ge(table_staged[x % STAGED], (x // STAGED + 1) * 32)
                nc.scalar.copy(table_hi[:, x, :], staged[x % STAGED]).then_inc(hi_made, 1)
                if x >= 3:
                    store_look_up(0, 0, x - 3)
            store_dense(0, use=0, bank=0)
            step(0, 0)
            act.wait_ge(memory_cleared, 2)
            store_dots(0, 0)
            step(0, 1)
            store_dots(0, 1)
            store_dense(2, use=1, bank=1)
            step(0, 2)
            act.wait_ge(weights_loaded, WEIGHT_LOADS * 16)
            with act.Fori(0, GROUPS - 1) as g:
                store_dots(g, 2)
                store_layer_1(g, 0, range(H1C - 1), **WHOLE)
                step(g, 3)
                store_layer_1(g, 0, (H1C - 1,), **WHOLE)
                store_dots(g, 3)
                store_next_dense(g, 0)
                store_layer_2(g, 0, **WHOLE)
                step(g + 1, 0)
                store_layer_3(g, 0, **WHOLE)
                store_dots(g + 1, 0)
                store_layer_1(g, 2, range(H1C - 1), **WHOLE)
                step(g + 1, 1)
                store_layer_1(g, 2, (H1C - 1,), **WHOLE)
                store_dots(g + 1, 1)
                store_next_dense(g, 2)
                store_layer_2(g, 2, **WHOLE)
                step(g + 1, 2)
                store_layer_3(g, 2, **WHOLE)
            g, t = LAST
            store_dots(g, 2)
            store_features(g, t, 0)
            store_features(g, t, 1)
            store_layer_1(g, 0, range(H1C), **LAST_DUO_BUT_ONE)
            store_features(g, t, 2)
            store_features(g, t, 3)
            store_layer_2(g, 0, **LAST_DUO_BUT_ONE)
            store_features(g, t, NB - 1, bank=0)
            store_layer_1(g, 2, (0, 1), **LAST_TILE_BUT_ONE)
            store_dots(g, t)
            store_layer_1(g, 2, (2, 3), **LAST_TILE_BUT_ONE)
            store_layer_3(g, 0, **LAST_DUO_BUT_ONE)
            store_layer_2(g, 2, **LAST_TILE_BUT_ONE)
            store_layer_1(g, t, range(H1C), **LAST_TILE)
            store_layer_3(g, 2, **LAST_TILE_BUT_ONE)
            store_layer_2(g, t, **LAST_TILE)
            store_layer_3(g, t, **LAST_TILE)
            act.wait_ge(layer_stored, uses_before(g, t) + LAST_USE + 1)
            act.dma_start(out, y_sb[:]).then_inc(out_stored, 16)
            act.wait_ge(out_stored, 16)

        @block.vector
        def _(dve):
            def start_onehot(g, t, k):
                h = k // HALF
                before = looked_up_before(g, t, k)
                dve.wait_ge(ids_loaded[h], (g * TILES + t + 1) * 16)
                if counts(lookup_freed(g, t, k)):
                    dve.wait_ge(looked_up, lookup_freed(g, t, k))

            def make_onehot(g, t, k, n):
                return nc.vector.tensor_scalar(onehot[:, lookup_slot(g, t, k), n, :],
                                               ids[k // HALF][0:KP, k % HALF, :],
                                               row_numbers[:, n:n + 1], None, ALU.is_equal)

            def whole_onehot(g, t, k):
                start_onehot(g, t, k)
                for n in range(KT):
                    last = make_onehot(g, t, k, n)
                last.then_inc(onehot_made, 1)

            def store_dots(g, t, i):
                tile = g * TILES + t
                dve.wait_ge(dots_done, tile * GB + i + 1)
                for j in DVE_BLOCKS:
                    last = nc.vector.tensor_copy(dots[B * j:B * j + FM, i * QB:(i + 1) * QB, :], dots_block(i, j))
                last.then_inc(dots_stored_dve, 1)

            def turn_dots(g, t):
                tile = g * TILES + t
                dve.wait_ge(dots_stored_act, (tile + 1) * GB)
                dve.wait_ge(dots_stored_dve, (tile + 1) * GB)
                nc.vector.transpose(turned[:, :, :], dots[:, :, :].rearrange("p q i -> p i q")
                                    ).then_inc(dots_turned, 1)

            def pack_pairs(g, t, features):
                tile = g * TILES + t
                if features[0] == 0:
                    dve.wait_ge(dots_turned, tile + 1)
                    if counts(tile):
                        dve.wait_ge(pairs_transposed, tile)
                for i in features:
                    last = nc.vector.tensor_copy(pairs[:, PAIR_AT[i]:PAIR_AT[i + 1]], turned[:, i, i:FM])
                if features[-1] == FM - 1:
                    last.then_inc(pairs_packed, 1)

            def store_pairs_t(g, t, bank=0):
                tile = g * TILES + t
                dve.wait_ge(pairs_transposed, tile + 1)
                for c in range(0, len(ZC), 2):
                    n = ZC[c][1]
                    cs = min(2, len(ZC) - c)
                    last = nc.vector.tensor_copy(
                        pairs_t[0:n, c:c + cs, t * P:(t + 1) * P],
                        transpose_banks[bank][0:n, c * P:(c + cs) * P].rearrange("p (c s) -> p c s", c=cs))
                last.then_inc(pairs_t_stored, 1)

            def step(g, t, dots_of, pairs_of=None, look_ups=True):
                ahead = after(g, t)
                parts = iter([(k, n) for k in range(2) for n in range(KT)] if look_ups else ())

                def some_onehots(count):
                    for _, (k, n) in zip(range(count), parts):
                        if n == 0:
                            start_onehot(*ahead, k)
                        last = make_onehot(*ahead, k, n)
                        if n == KT - 1:
                            last.then_inc(onehot_made, 1)

                some_onehots(4)
                if pairs_of is not None:
                    store_pairs_t(*pairs_of)
                for i in range(GB):
                    store_dots(*dots_of, i)
                    some_onehots(2 - i % 2)
                turn_dots(*dots_of)
                pack_pairs(*dots_of, range(FM // 2))
                if look_ups:
                    for k in range(2, len(chunk(*ahead))):
                        whole_onehot(*ahead, k)
                pack_pairs(*dots_of, range(FM // 2, FM))

            nc.vector.memset(dots[:], 0.0).then_inc(memory_cleared, 1)
            nc.vector.memset(rows_t[:, :, :, :, F:B], 0.0).then_inc(memory_cleared, 1)
            dve.wait_ge(numbers_loaded, 16)

            def make_lo(x):
                dve.wait_ge(table_staged[x % STAGED], (x // STAGED + 1) * 32)
                dve.wait_ge(hi_made, x + 1)
                nc.vector.tensor_tensor(table_lo[:, x, :], staged[x % STAGED], table_hi[:, x, :].bitcast(f32),
                                        ALU.subtract).then_inc(lo_made, 1)

            for t in range(2):
                for k, x in enumerate(chunk(0, t)):
                    make_lo(x)
                    whole_onehot(0, t, k)
            dve.wait_ge(weights_loaded, WEIGHT_LOADS * 16)
            nc.vector.tensor_tensor(w1_sb[:, 0, :], w1_sb[:, 0, :], w1_dense2, ALU.add
                                    ).then_inc(dense_weights_summed, 1)
            step(0, 1, (0, 0))
            step(0, 2, (0, 1), (0, 0))
            with dve.Fori(0, GROUPS - 1) as g:
                step(g, 3, (g, 2), (g, 1))
                step(g + 1, 0, (g, 3), (g, 2))
                step(g + 1, 1, (g + 1, 0), (g, 3))
                step(g + 1, 2, (g + 1, 1), (g + 1, 0))
            g, t = LAST
            step(g, t, (g, 2), (g, 1), look_ups=False)
            store_pairs_t(g, 2, bank=1)
            for i in range(GB):
                store_dots(g, t, i)
            turn_dots(g, t)
            pack_pairs(g, t, range(FM))
            store_pairs_t(g, t, bank=1)


def kernel(**inputs):
    import numpy as np
    import concourse.bacc as bacc
    from concourse.bass_utils import run_bass_kernel_spmd

    def pair_row(i, j):
        a, b = sorted((ORDER[i], ORDER[j]))
        return P + a * (F - 1) - a * (a - 1) // 2 + b - a - 1

    w1_rows = list(range(P)) + list(range(P + PAIRS, P + PAIRS + P))
    w1_rows += [pair_row(i, j) for i in range(F) for j in range(i + 1, F)]
    ids = np.asarray(inputs["ids"])
    arrays = {
        "dense": np.asarray(inputs["r_dense_features"]),
        "ids_tiles": ids.reshape(BATCH // P, P, NUM_TABLES),
        "ids_rows": ids.T[list(LOOKED_UP)],
        "w1": np.asarray(inputs["W_top1"])[w1_rows],
        "b1": np.asarray(inputs["b_top1"]).reshape(H1C, P).T,
        "w2": np.asarray(inputs["W_top2"]),
        "b2": np.asarray(inputs["b_top2"]).reshape(H2C, P).T,
        "w3": np.asarray(inputs["W_top3"]).reshape(H2C, P).T,
        "identity": np.eye(P, dtype=np.float32),
        "row_numbers": np.arange(ROWS, dtype=np.float32).reshape(KP, KT),
    }
    for f in range(NUM_TABLES):
        arrays[f"tbl_{f}"] = np.asarray(inputs[f"tbl_{f}"])
    arrays = {f"in_{k}": np.ascontiguousarray(a) for k, a in arrays.items()}

    nc = bacc.Bacc("TRN2", target_bir_lowering=False, num_devices=1)
    ap = {k[3:]: nc.dram_tensor(k, a.shape, mybir.dt.from_np(a.dtype), kind="ExternalInput").ap()
          for k, a in arrays.items()}
    out = nc.dram_tensor("out", [P, ALL_TILES], mybir.dt.float32, kind="ExternalOutput").ap()
    dlrm_kernel(nc, ap["dense"], ap["ids_tiles"], ap["ids_rows"], [ap[f"tbl_{f}"] for f in GATHERED],
                [ap[f"tbl_{f}"] for f in LOOKED_UP], ap["w1"], ap["b1"], ap["w2"], ap["b2"], ap["w3"],
                ap["identity"], ap["row_numbers"], out)
    result = run_bass_kernel_spmd(nc, [arrays], core_ids=[0])
    return result.results[0]["out"].T.reshape(BATCH, 1)
```
